# Optimizing a Trainium2 kernel written in Bass

```python
import numpy as np
import jax
import jax.numpy as jnp

def _softmax(x, axis=-1):
    return jax.nn.softmax(x, axis=axis)

def _gelu(x):
    return jax.nn.gelu(x, approximate=True)

def _silu(x):
    return jax.nn.silu(x)

def _sigmoid(x):
    return jax.nn.sigmoid(x)

def _layernorm(x, axis=-1, eps=1e-05):
    m = jnp.mean(x, axis=axis, keepdims=True)
    v = jnp.var(x, axis=axis, keepdims=True)
    return (x - m) / jnp.sqrt(v + eps)

def _scatter_add(tgt, idx, src, axis=0):
    return tgt.at[idx].add(src)

def _segment_sum(src, seg, n):
    return jax.ops.segment_sum(src, seg, n)
kernel_name = 'mk_gnn_resnorm_d2_gnn_r8_b8e7d2'

def setup_inputs(seed: int=0):
    np.random.seed(seed)
    _w = jnp.asarray

    def _rec_inputs():
        import jax
        import jax.numpy as jnp
        _gk = jax.random.key(seed)
        x = -0.000202 + 1 * jax.random.normal(jax.random.fold_in(_gk, 1), (12500, 64), jnp.float32)
        src = jax.random.randint(jax.random.fold_in(_gk, 2), (400000,), 0, 12500, jnp.int32)
        dst = jax.random.randint(jax.random.fold_in(_gk, 3), (400000,), 0, 12500, jnp.int32)
        _o = jnp.argsort(dst, stable=True)
        src = src[_o]
        dst = dst[_o]
        edge_attr_128 = jax.random.uniform(jax.random.fold_in(_gk, 12), (400000, 128), jnp.float32, 0.0, 1)
        return (x, src, dst, edge_attr_128)
    x, src, dst, edge_attr_128 = _rec_inputs()

    def _L0_gnn_setup():
        import jax, jax.numpy as jnp
        import numpy as np
        N_NODES = 12500
        D_IN = 64
        D_HID = 128
        key = jax.random.key(seed)
        k_x, k_e, k_w1, k_b1, k_w2, k_b2 = jax.random.split(key, 6)
        x = jax.random.normal(k_x, (N_NODES, D_IN), dtype=jnp.float32)
        edge_index = jax.random.randint(k_e, (2, 200000), 0, N_NODES, dtype=jnp.int64)
        s1 = 1.0 / np.sqrt(D_IN)
        s2 = 1.0 / np.sqrt(D_HID)
        W1 = jax.random.uniform(k_w1, (D_IN, D_HID), jnp.float32, -s1, s1)
        b1 = jax.random.uniform(k_b1, (D_HID,), jnp.float32, -s1, s1)
        W2 = jax.random.uniform(k_w2, (D_HID, D_IN), jnp.float32, -s2, s2)
        b2 = jax.random.uniform(k_b2, (D_IN,), jnp.float32, -s2, s2)
        return {'x': x, 'edge_index': edge_index, 'W1': W1, 'b1': b1, 'W2': W2, 'b2': b2}
    _L0_gnn_all = _L0_gnn_setup()
    _L0_gnn_in = {k: v for k, v in _L0_gnn_all.items() if k in ('W1', 'b1', 'W2', 'b2')}
    del _L0_gnn_all

    def _L1_gnn_setup():
        import jax, jax.numpy as jnp
        import numpy as np
        N_NODES = 12500
        N_EDGES = 100000
        DIM = 64
        RBF_DIM = 128

        def ssp(x):
            return jnp.where(0.5 * x > 14.0, x, 2.0 * jnp.logaddexp(0.0, 0.5 * x))
        key = jax.random.key(seed)
        ks = jax.random.split(key, 16)
        s = 1.0 / np.sqrt(DIM)
        sr = 1.0 / np.sqrt(RBF_DIM)
        return {'node': jax.random.normal(ks[0], (N_NODES, DIM), dtype=jnp.float32), 'rbf': jax.random.uniform(ks[1], (N_EDGES, RBF_DIM), dtype=jnp.float32), 'src': jax.random.randint(ks[2], (N_EDGES,), 0, N_NODES), 'dst': jax.random.randint(ks[3], (N_EDGES,), 0, N_NODES), 'W1': jax.random.uniform(ks[4], (DIM, DIM), jnp.float32, -s, s), 'Wc1': jax.random.uniform(ks[5], (DIM, RBF_DIM), jnp.float32, -sr, sr), 'bc1': jax.random.uniform(ks[6], (DIM,), jnp.float32, -sr, sr), 'Wc2': jax.random.uniform(ks[7], (DIM, DIM), jnp.float32, -s, s), 'bc2': jax.random.uniform(ks[8], (DIM,), jnp.float32, -s, s), 'W2': jax.random.uniform(ks[9], (DIM, DIM), jnp.float32, -s, s), 'b2': jax.random.uniform(ks[10], (DIM,), jnp.float32, -s, s), 'W3': jax.random.uniform(ks[11], (DIM, DIM), jnp.float32, -s, s), 'b3': jax.random.uniform(ks[12], (DIM,), jnp.float32, -s, s)}
    _L1_gnn_all = _L1_gnn_setup()
    _L1_gnn_in = {k: v for k, v in _L1_gnn_all.items() if k in ('W1', 'Wc1', 'bc1', 'Wc2', 'bc2', 'W2', 'b2', 'W3', 'b3')}
    del _L1_gnn_all
    return {'x': x, 'src': src, 'dst': dst, 'edge_attr_128': edge_attr_128, 'L0_gnn_W1': _L0_gnn_in['W1'], 'L0_gnn_b1': _L0_gnn_in['b1'], 'L0_gnn_W2': _L0_gnn_in['W2'], 'L0_gnn_b2': _L0_gnn_in['b2'], 'L1_gnn_W1': _L1_gnn_in['W1'], 'L1_gnn_Wc1': _L1_gnn_in['Wc1'], 'L1_gnn_bc1': _L1_gnn_in['bc1'], 'L1_gnn_Wc2': _L1_gnn_in['Wc2'], 'L1_gnn_bc2': _L1_gnn_in['bc2'], 'L1_gnn_W2': _L1_gnn_in['W2'], 'L1_gnn_b2': _L1_gnn_in['b2'], 'L1_gnn_W3': _L1_gnn_in['W3'], 'L1_gnn_b3': _L1_gnn_in['b3']}

def reference(x, src, dst, edge_attr_128, L0_gnn_W1, L0_gnn_b1, L0_gnn_W2, L0_gnn_b2, L1_gnn_W1, L1_gnn_Wc1, L1_gnn_bc1, L1_gnn_Wc2, L1_gnn_bc2, L1_gnn_W2, L1_gnn_b2, L1_gnn_W3, L1_gnn_b3):
    import jax
    import jax.numpy as jnp

    def _L0_gnn_ref(x, edge_index, W1, b1, W2, b2):
        import jax, jax.numpy as jnp
        import numpy as np
        N_NODES = 12500
        D_IN = 64
        D_HID = 128
        row, col = (edge_index[0], edge_index[1])
        agg = jax.ops.segment_sum(x[col], row, num_segments=x.shape[0])
        out = agg + x
        h = jax.nn.relu(out @ W1 + b1)
        return h @ W2 + b2

    def _L1_gnn_ref(node, rbf, src, dst, W1, Wc1, bc1, Wc2, bc2, W2, b2, W3, b3):
        import jax, jax.numpy as jnp
        import numpy as np
        N_NODES = 12500
        N_EDGES = 100000
        DIM = 64
        RBF_DIM = 128

        def ssp(x):
            return jnp.where(0.5 * x > 14.0, x, 2.0 * jnp.logaddexp(0.0, 0.5 * x))
        new_node = node @ W1.T
        h = ssp(rbf @ Wc1.T + bc1) @ Wc2.T + bc2
        msg = new_node[src] * h
        cf_node = jax.ops.segment_sum(msg, dst, num_segments=node.shape[0])
        out = node + ssp(cf_node @ W2.T + b2) @ W3.T + b3 * 0 + (ssp(cf_node @ W2.T + b2) @ W3.T + b3 - ssp(cf_node @ W2.T + b2) @ W3.T)
        out = node + (ssp(cf_node @ W2.T + b2) @ W3.T + b3)
        return out
    edge_index = jnp.stack([src, dst])
    x = _layernorm(x + _L0_gnn_ref(x, edge_index, L0_gnn_W1, L0_gnn_b1, L0_gnn_W2, L0_gnn_b2), axis=-1)
    x = _layernorm(x + _L1_gnn_ref(x, edge_attr_128, src, dst, L1_gnn_W1, L1_gnn_Wc1, L1_gnn_bc1, L1_gnn_Wc2, L1_gnn_bc2, L1_gnn_W2, L1_gnn_b2, L1_gnn_W3, L1_gnn_b3), axis=-1)
    return x

_drawn_inputs = setup_inputs


def setup_inputs(seed=0):
    import zlib

    import numpy as np

    out = dict(_drawn_inputs(seed))
    spreads = {}
    factors = {'edge_attr_128': 4.615, 'L1_gnn_bc1': 4.644, 'L1_gnn_b2': 6.043}
    for name, (base, spread) in spreads.items():
        noise = np.random.default_rng([zlib.crc32(name.encode()), seed]).standard_normal(out[name].shape)
        drawn = base * np.exp(spread * noise) if base else spread * noise
        out[name] = jnp.asarray(drawn.astype(out[name].dtype))
    for name, factor in factors.items():
        out[name] = (out[name] * factor).astype(out[name].dtype)
    return out
```

```python
from contextlib import ExitStack

import concourse.bass as bass
from concourse import mybir

F32 = mybir.dt.float32
BF16 = mybir.dt.bfloat16
I32 = mybir.dt.int32
ALU = mybir.AluOpType
ACT = mybir.ActivationFunctionType
AX_X = mybir.AxisListType.X

P = 128
GT = 5
GR = 5
CT = GT * GR
WIN = 128
ACCS = 5
BT = 7
EPS = 1e-5
CAP = 20.0
BANK = 512


def bcast(ap, axis, n):
    shape = list(ap.shape)
    return ap.unsqueeze(axis).broadcast_to(shape[:axis] + [n] + shape[axis:])


def wait_alone(eng, sem, value, turn):
    eng.wait_ge(sem, value)
    eng.sem_inc(turn, 1)


class Plan:
    pass


def make_plan(nc, ctx, ins, out):
    g = Plan()
    g.ins, g.out = ins, out
    g.N, g.D = ins["x"].shape
    g.E, g.F = ins["edge_attr_128"].shape
    g.HID = ins["L0_gnn_W1"].shape[1]
    g.NC = g.E // (P * CT)
    g.NT = -(-g.N // P)
    g.NB = g.NT // BT
    g.NW = -(-g.N // WIN)
    g.ROWS = P * (g.NT + 1)
    assert g.E == g.NC * P * CT and g.NT == g.NB * BT and g.NB % 2 == 0
    assert g.ROWS >= g.N + P and g.ROWS >= g.N + WIN and g.D == 64 and g.F == P and g.HID == P
    assert g.NC <= P

    def dram(name, cols, dt):
        return nc.dram_tensor(name, (g.ROWS, cols), dt, kind="Internal").ap()

    g.acc = [dram(f"agg_part{k}", g.D, F32) for k in range(ACCS)]
    g.cf = dram("cf_node", g.D, F32)
    g.nn = dram("new_node", g.D, F32)
    g.xs = dram("x_split", 3 * g.D, BF16)

    def sb(name, shape, dt):
        return ctx.enter_context(nc.sbuf_tensor(name, shape, dt))

    g.identF = sb("identF", [P, P], F32)
    g.identB = sb("identB", [P, P], BF16)
    g.iota_w = sb("iota_w", [P, WIN], F32)
    g.win_off = sb("win_off", [P, g.NW], F32)
    g.pow_col = sb("pow_col", [P, 1], BF16)
    g.pow_lim = sb("pow_lim", [P, 1], F32)
    g.trash = sb("trash", [P, 1], F32)
    g.sel = sb("sel", [2 * CT, CT, P], BF16)
    g.ones = sb("ones", [1, P], F32)
    g.srcF = sb("srcF", [P, g.NC, CT], F32)
    g.dstF = sb("dstF", [P, g.NC, CT], F32)
    g.src_hl = sb("src_hl", [P, g.NC, 2 * CT], BF16)
    g.minB = sb("minB", [P, g.NC], F32)
    g.tab_min = sb("tab_min", [P, g.NC], I32)
    g.tab_nw = sb("tab_nw", [P, g.NC], I32)
    g.xres = sb("xres", [P, g.NT * g.D], F32)
    g.W1 = sb("W1", [g.D, g.HID], F32)
    g.b1 = sb("b1", [g.HID, 1], F32)
    g.W2 = sb("W2", [g.HID, g.D], F32)
    g.b2rep = sb("b2rep", [1, BT, g.D], F32)
    g.V1T = sb("V1T", [g.D, g.D], F32)
    g.Wc1T = sb("Wc1T", [g.F, g.D], F32)
    g.bc1h = sb("bc1h", [P, 1], F32)
    g.Wc2d = sb("Wc2d", [P, 2, g.D], F32)
    g.bc2p = sb("bc2p", [3, GT, g.D], BF16)
    g.ones3 = sb("ones3", [3, P], BF16)
    g.V2T = sb("V2T", [g.D, g.D], F32)
    g.v2h = sb("v2h", [g.D, 1], F32)
    g.V3T = sb("V3T", [g.D, g.D], F32)
    g.v3rep = sb("v3rep", [1, BT, g.D], F32)
    g.acc_done = [ctx.enter_context(nc.semaphore(f"acc_done{k}")) for k in range(ACCS)]
    g.pool_turn = ctx.enter_context(nc.semaphore("pool_turn"))
    g.sp_turn = ctx.enter_context(nc.semaphore("sp_turn"))
    g.pe_turn = ctx.enter_context(nc.semaphore("pe_turn"))
    return g


def load_nodes(eng, g, tile, dram, sem, store=False):
    row = g.NT * g.D
    full = g.N // g.NT
    even = full // 16 * 16
    rest = (g.N - full * g.NT) * g.D
    whole = dram[0:full * g.NT, :].rearrange("(p t) d -> p (t d)", t=g.NT)
    last = dram[full * g.NT:g.N, :].rearrange("(o t) d -> o (t d)", o=1)
    for s, d in ((tile[0:even, :], whole[0:even, :]), (tile[even:full, :], whole[even:full, :]),
                 (tile[full:full + 1, 0:rest], last)):
        eng.dma_start(d if store else s, s if store else d).then_inc(sem, 16)
    assert full + 1 == P and row == tile.shape[1]


def prep_phase(nc, g):
    ins = g.ins
    with ExitStack() as ctx:
        def sb(name, shape, dt):
            return ctx.enter_context(nc.sbuf_tensor(name, shape, dt))

        def sem(name):
            return ctx.enter_context(nc.semaphore(name))

        zeros = sb("zeros", [P, g.ROWS // P * g.D], F32)
        idx_i = sb("idx_i", [P, 2, g.NC, CT], I32)
        parts = sb("parts", [P, 2, BT, 3, g.D], BF16)
        left = sb("left", [P, 2, BT, 2, g.D], F32)
        int_c = sb("int_c", [P, WIN + g.NW + 3], I32)
        wload = sb("wload", [g.D, 5, P], F32)
        ext = sb("ext", [P, 2, g.NC], F32)
        colx = sb("colx", [P, 2], F32)
        colb = sb("colb", [P, 2, P], F32)
        bc2rep = sb("bc2rep", [1, GT, g.D], F32)
        bc2part = sb("bc2part", [1, 3, GT, g.D], BF16)
        bc2left = sb("bc2left", [1, 2, GT, g.D], F32)
        ps_t = ctx.enter_context(nc.psum_tensor("prep_t", [P, 2, BANK], F32))
        ps_w = ctx.enter_context(nc.psum_tensor("prep_w", [P, 5, P], F32))

        x_in = sem("x_in")
        src_in = sem("src_in")
        dst_in = sem("dst_in")
        w_in = sem("w_in")
        rep_in = sem("rep_in")
        zeroed = sem("zeroed")
        x_padded = sem("x_padded")
        const_set = sem("const_set")
        const_sel = sem("const_sel")
        iota_done = sem("iota_done")
        v_step = sem("v_step")
        ext_ready = sem("ext_ready")
        ext_turned = sem("ext_turned")
        col_ready = sem("col_ready")
        ext_spread = sem("ext_spread")
        w_turned = sem("w_turned")
        part_ready = sem("part_ready")
        part_free = [sem(f"part_free{h}") for h in range(2)]
        xs_pad = sem("xs_pad")
        bias_split = sem("bias_split")
        bias_in = sem("bias_in")
        cf_zero = sem("cf_zero")

        src_v = ins["src"].rearrange("(c p t) -> p c t", p=P, t=CT)
        dst_v = ins["dst"].rearrange("(c p t) -> p c t", p=P, t=CT)
        xs_v = g.xs[0:P * g.NT, :].rearrange("(p t) d -> p (t d)", t=g.NT)

        block = ctx.enter_context(nc.Block())

        @block.sync
        def _(sp):
            sp.dma_start(idx_i[:, 1, :, :], dst_v).then_inc(dst_in, 16)
            sp.dma_start(idx_i[:, 0, :, :], src_v).then_inc(src_in, 16)
            sp.wait_ge(x_padded, 1)
            load_nodes(sp, g, g.xres, ins["x"], x_in)
            sp.wait_ge(zeroed, 1)
            for b in range(g.NT // BT):
                h = b % 2
                sp.wait_ge(part_ready, b + 1)
                sp.dma_start(xs_v[:, b * BT * 3 * g.D:(b + 1) * BT * 3 * g.D],
                             parts[:, h].rearrange("p t a d -> p (t a d)")).then_inc(part_free[h], 16)
            sp.dma_start(g.cf.rearrange("(p t) d -> p (t d)", p=P), zeros[:, :]).then_inc(cf_zero, 16)
            sp.dma_start(g.xs[P * g.NT:g.ROWS, :].bitcast(F32),
                         zeros[:, 0:3 * g.D // 2]).then_inc(xs_pad, 16)
            for h in range(2):
                sp.wait_ge(part_free[h], 16 * (g.NT // BT // 2))
            sp.wait_ge(xs_pad, 16)
            sp.wait_ge(cf_zero, 16)

        @block.scalar
        def _(act):
            def small(out, in_):
                act.dma_start(out, in_).then_inc(w_in, 16)

            def column(v):
                return v.rearrange("(n o) -> n o", o=1)

            def row(v):
                return v.rearrange("(o n) -> o n", o=1)

            small(g.W1[:, :], ins["L0_gnn_W1"])
            small(g.W2[:, :], ins["L0_gnn_W2"])
            small(g.b1[:, :], column(ins["L0_gnn_b1"]))
            small(wload[:, 0, 0:g.D], ins["L1_gnn_W1"])
            small(wload[:, 1, :], ins["L1_gnn_Wc1"])
            small(wload[:, 2, 0:g.D], ins["L1_gnn_Wc2"])
            small(wload[:, 2, g.D:P], ins["L1_gnn_Wc2"])
            small(wload[:, 3, 0:g.D], ins["L1_gnn_W2"])
            small(wload[:, 4, 0:g.D], ins["L1_gnn_W3"])
            small(g.bc1h[0:g.D, :], column(ins["L1_gnn_bc1"]))
            small(g.bc1h[g.D:P, :], column(ins["L1_gnn_bc1"]))
            small(g.v2h[:, :], column(ins["L1_gnn_b2"]))
            for t in range(BT):
                act.dma_start(g.b2rep[:, t, :], row(ins["L0_gnn_b2"])).then_inc(rep_in, 16)
                act.dma_start(g.v3rep[:, t, :], row(ins["L1_gnn_b3"])).then_inc(rep_in, 16)
            for t in range(GT):
                act.dma_start(bc2rep[:, t, :], row(ins["L1_gnn_bc2"])).then_inc(rep_in, 16)
            act.wait_ge(bias_split, 1)
            for k in range(3):
                act.dma_start(g.bc2p[k:k + 1, :, :], bc2part[:, k, :, :]).then_inc(bias_in, 16)
            act.wait_ge(bias_in, 48)

        @block.gpsimd
        def _(pool):
            nc.gpsimd.memset(g.identF[:, :], 0.0).then_inc(const_set, 1)
            nc.gpsimd.memset(g.identB[:, :], 0.0).then_inc(const_set, 1)
            nc.gpsimd.memset(g.sel[:, :, :], 0.0).then_inc(const_set, 1)
            nc.gpsimd.memset(g.ones[:, :], 1.0).then_inc(const_set, 1)
            nc.gpsimd.memset(g.ones3[:, :], 1.0).then_inc(const_set, 1)
            o = WIN + g.NW
            nc.gpsimd.iota(int_c[:, 0:WIN], [[1, WIN]], 0, 0).then_inc(iota_done, 1)
            nc.gpsimd.iota(int_c[:, WIN:o], [[WIN, g.NW]], 0, 0).then_inc(iota_done, 1)
            nc.gpsimd.iota(int_c[:, o:o + 1], [[0, 1]], g.N, 1).then_inc(iota_done, 1)
            nc.gpsimd.iota(int_c[:, o + 1:o + 2], [[0, 1]], (127 + 63) << 23, -(1 << 23)).then_inc(iota_done, 1)
            nc.gpsimd.iota(int_c[:, o + 2:o + 3], [[0, 1]], ((127 + 64) << 23) + (1 << 21), -(1 << 23)).then_inc(iota_done, 1)
            pool.wait_ge(const_set, 5)
            nc.gpsimd.affine_select(out=g.identF[:, :], in_=g.identF[:, :], compare_op=ALU.not_equal, fill=1.0,
                                    base=0, pattern=[[-1, P]], channel_multiplier=1).then_inc(const_sel, 1)
            nc.gpsimd.affine_select(out=g.identB[:, :], in_=g.identB[:, :], compare_op=ALU.not_equal, fill=1.0,
                                    base=0, pattern=[[-1, P]], channel_multiplier=1).then_inc(const_sel, 1)
            nc.gpsimd.affine_select(out=g.sel[:, :, :], in_=g.sel[:, :, :], compare_op=ALU.not_equal, fill=128.0,
                                    base=0, pattern=[[-1, CT], [0, P]], channel_multiplier=1).then_inc(const_sel, 1)
            pool.wait_ge(const_sel, 3)
            nc.gpsimd.affine_select(out=g.sel[:, :, :], in_=g.sel[:, :, :], compare_op=ALU.not_equal, fill=1.0,
                                    base=-CT, pattern=[[-1, CT], [0, P]], channel_multiplier=1).then_inc(const_sel, 1)
            pool.wait_ge(zeroed, 1)
            for k in range(ACCS):
                pool.dma_start(g.acc[k].rearrange("(p t) d -> p (t d)", p=P), zeros[:, :]).then_inc(g.acc_done[k], 16)
            for k in range(ACCS):
                pool.wait_ge(g.acc_done[k], 16)

        @block.vector
        def _(dve):
            steps = [0]

            def then(ins_):
                steps[0] += 1
                ins_.then_inc(v_step, 1)
                dve.wait_ge(v_step, steps[0])

            nc.vector.memset(g.xres[96:P, :], 0.0).then_inc(x_padded, 1)
            nc.vector.memset(zeros[:, :], 0.0).then_inc(zeroed, 1)
            dve.wait_ge(dst_in, 16)
            then(nc.vector.tensor_copy(g.dstF[:, :, :], idx_i[:, 1, :, :]))
            nc.vector.tensor_reduce(ext[:, 0, :], g.dstF[:, :, :], AX_X, ALU.min).then_inc(ext_ready, 1)
            nc.vector.tensor_reduce(ext[:, 1, :], g.dstF[:, :, :], AX_X, ALU.max).then_inc(ext_ready, 1)
            dve.wait_ge(src_in, 16)
            nc.vector.tensor_copy(g.srcF[:, :, :], idx_i[:, 0, :, :])
            then(nc.vector.tensor_single_scalar(idx_i[:, 1, :, :], idx_i[:, 0, :, :], 7, ALU.arith_shift_right))
            then(nc.vector.tensor_copy(g.src_hl[:, :, 0:CT], idx_i[:, 1, :, :]))
            then(nc.vector.tensor_single_scalar(idx_i[:, 1, :, :], idx_i[:, 0, :, :], 127, ALU.bitwise_and))
            nc.vector.tensor_copy(g.src_hl[:, :, CT:2 * CT], idx_i[:, 1, :, :])
            dve.wait_ge(ext_turned, 1)
            nc.vector.tensor_reduce(colx[0:g.NC, 0:1], ps_t[0:g.NC, 0, 0:P], AX_X, ALU.min)
            then(nc.vector.tensor_reduce(colx[0:g.NC, 1:2], ps_t[0:g.NC, 1, 0:P], AX_X, ALU.max))
            then(nc.vector.tensor_copy(colb[0:g.NC, :, :], bcast(colx[0:g.NC, :], 2, P)))
            nc.vector.tensor_copy(colb[0:g.NC, 0, 0:1], colx[0:g.NC, 0:1]).then_inc(col_ready, 1)
            dve.wait_ge(ext_spread, 1)
            nc.vector.tensor_copy(g.minB[:, :], ps_t[:, 0, 0:g.NC])
            nc.vector.tensor_copy(g.tab_min[:, :], ps_t[:, 0, 0:g.NC])
            then(nc.vector.tensor_copy(g.tab_nw[:, :], ps_t[:, 1, 0:g.NC]))
            then(nc.vector.tensor_tensor(g.tab_nw[:, :], g.tab_nw[:, :], g.tab_min[:, :], ALU.subtract))
            then(nc.vector.tensor_single_scalar(g.tab_nw[:, :], g.tab_nw[:, :], 7, ALU.arith_shift_right))
            nc.vector.tensor_single_scalar(g.tab_nw[:, :], g.tab_nw[:, :], 1, ALU.add)
            o = WIN + g.NW
            dve.wait_ge(iota_done, 5)
            nc.vector.tensor_copy(g.iota_w[:, :], int_c[:, 0:WIN])
            nc.vector.tensor_copy(g.win_off[:, :], int_c[:, WIN:o])
            nc.vector.tensor_copy(g.trash[:, :], int_c[:, o:o + 1])
            nc.vector.tensor_copy(g.pow_col[:, :], int_c[:, o + 1:o + 2].bitcast(F32))
            nc.vector.tensor_copy(g.pow_lim[:, :], int_c[:, o + 2:o + 3].bitcast(F32))
            dve.wait_ge(w_turned, 1)
            nc.vector.tensor_copy(g.V1T[:, :], ps_w[0:g.D, 0, 0:g.D])
            nc.vector.tensor_scalar_mul(g.Wc1T[:, :], ps_w[:, 1, 0:g.D], 0.5)
            for k in range(2):
                lo = slice(k * g.D, (k + 1) * g.D)
                nc.vector.memset(g.Wc2d[lo, 1 - k, :], 0.0)
                nc.vector.tensor_scalar_mul(g.Wc2d[lo, k, :], ps_w[lo, 2, 0:g.D], 2.0)
            nc.vector.tensor_scalar_mul(g.V2T[:, :], ps_w[0:g.D, 3, 0:g.D], 0.5)
            nc.vector.tensor_scalar_mul(g.V3T[:, :], ps_w[0:g.D, 4, 0:g.D], 2.0)
            nc.vector.tensor_scalar_mul(g.bc1h[:, :], g.bc1h[:, :], 0.5)
            nc.vector.tensor_scalar_mul(g.v2h[:, :], g.v2h[:, :], 0.5)
            def split(part, left_, value):
                then(nc.vector.tensor_copy(part[0], value))
                then(nc.vector.tensor_tensor(left_[0], value, part[0], ALU.subtract))
                then(nc.vector.tensor_copy(part[1], left_[0]))
                then(nc.vector.tensor_tensor(left_[1], left_[0], part[1], ALU.subtract))
                return nc.vector.tensor_copy(part[2], left_[1])

            dve.wait_ge(rep_in, 16 * (2 * BT + GT))
            split([bc2part[:, k] for k in range(3)], [bc2left[:, k] for k in range(2)],
                  bc2rep[:, :, :]).then_inc(bias_split, 1)
            dve.wait_ge(x_in, 48)
            xv = g.xres[:, :].rearrange("p (t d) -> p t d", d=g.D)
            for b in range(g.NT // BT):
                h = b % 2
                xb = xv[:, b * BT:(b + 1) * BT, :]
                if b >= 2:
                    dve.wait_ge(part_free[h], 16 * (b // 2))
                split([parts[:, h, :, k, :] for k in range(3)], [left[:, h, :, k, :] for k in range(2)],
                      xb).then_inc(part_ready, 1)

        @block.tensor
        def _(pe):
            pe.wait_ge(const_sel, 4)
            pe.wait_ge(w_in, 16 * 12)
            for i in range(5):
                n = P if i in (1, 2) else g.D
                last = nc.tensor.transpose(ps_w[0:n, i, 0:g.D], wload[:, i, 0:n], g.identF[0:g.D, 0:g.D])
            last.then_inc(w_turned, 1)
            pe.wait_ge(ext_ready, 2)
            nc.tensor.transpose(ps_t[0:g.NC, 0, 0:P], ext[:, 0, :], g.identF[:, :])
            nc.tensor.transpose(ps_t[0:g.NC, 1, 0:P], ext[:, 1, :], g.identF[:, :]).then_inc(ext_turned, 1)
            pe.wait_ge(col_ready, 1)
            for i in range(2):
                last = nc.tensor.matmul(ps_t[:, i, 0:g.NC], colb[0:g.NC, i, :], g.identF[0:g.NC, 0:g.NC],
                                        start=True, stop=True)
            last.then_inc(ext_spread, 1)


def each_unit(eng, g, name):
    done = eng.alloc_register(name)
    eng.reg_mov(done, 0)
    with eng.Fori(0, g.NC) as c:
        windows = eng.value_load(g.tab_nw[0:1, bass.ds(c, 1)], min_val=1, max_val=g.NW)
        with eng.Fori(0, windows) as w:
            yield c, w, eng.snap(done, min_val=0, max_val=g.NC * g.NW)
            eng.reg_add(done, done, 1)
    yield None, None, eng.snap(done, min_val=0, max_val=g.NC * g.NW)


def window_base(eng, g, c, w, name):
    first = eng.value_load(g.tab_min[0:1, bass.ds(c, 1)], min_val=0, max_val=g.N - 1)
    base = eng.alloc_register(name)
    eng.reg_mov(base, first + w * WIN)
    return eng.snap(base, min_val=0, max_val=g.N - 1)


def layer0_edges(nc, g):
    with ExitStack() as ctx:
        def sb(name, shape, dt):
            return ctx.enter_context(nc.sbuf_tensor(name, shape, dt))

        def ps(name, shape, dt):
            return ctx.enter_context(nc.psum_tensor(name, shape, dt))

        def sem(name):
            return ctx.enter_context(nc.semaphore(name))

        x_win = sb("x_win", [WIN, 3, g.D], BF16)
        cur_hl = sb("cur_hl", [P, 2 * CT], BF16)
        cur_src = sb("cur_src", [P, CT], F32)
        cur_dst = sb("cur_dst", [P, CT], F32)
        to_trash = sb("to_trash", [P, CT], F32)
        src_rows = sb("src_rows", [2 * CT, P], BF16)
        oh = sb("oh", [P, CT, WIN], BF16)
        eq = sb("eq", [P, CT, P], BF16)
        counts = sb("counts", [WIN, GT, P], BF16)
        moved = sb("moved", [P, CT], F32)
        target = sb("target", [P, CT], I32)
        rows = sb("rows", [P, CT, g.D], F32)
        ps_hl = ps("ps_hl", [2 * CT, P], BF16)
        ps_src = ps("ps_src", [P, 2 * BANK], F32)
        ps_cnt = ps("ps_cnt", [P, 2 * BANK], F32)
        ps_first = ps("ps_first", [P, BANK], F32)
        ps_rows = ps("ps_rows", [P, BANK], F32)
        spread = ps_src[:, 0:GT * P].rearrange("p (t e) -> p t e", t=GT)
        cnt = ps_cnt[:, 0:GT * P].rearrange("p (t e) -> p t e", t=GT)
        sums = ps_rows[:, 0:GT * g.D].rearrange("p (t d) -> p t d", t=GT)

        x_win_in = sem("x_win_in")
        cur_ready = sem("cur_ready")
        hl_turned = sem("hl_turned")
        hl_copied = sem("hl_copied")
        spread_done = sem("spread_done")
        eq_ready = sem("eq_ready")
        cnt_done = sem("cnt_done")
        cnt_copied = sem("cnt_copied")
        sums_done = sem("sums_done")
        rows_ready = sem("rows_ready")
        mark_ready = sem("mark_ready")
        target_ready = sem("target_ready")
        rows_free = sem("rows_free")

        block = ctx.enter_context(nc.Block())

        @block.sync
        def _(sp):
            for c, w, u in each_unit(sp, g, "sp_unit"):
                if c is None:
                    continue
                base = window_base(sp, g, c, w, "sp_base")
                sp.wait_ge(sums_done, u * GR + GR)
                sp.dma_start(x_win[:, :, :].rearrange("p a d -> p (a d)"),
                             g.xs[bass.ds(base, WIN), :]).then_inc(x_win_in, 16)

        @block.vector
        def _(dve):
            def one_hot(j):
                t = slice(j * GT, (j + 1) * GT)
                return nc.vector.tensor_tensor(oh[:, t, :], bcast(g.iota_w[:, :], 1, GT),
                                               bcast(cur_dst[:, t], 2, WIN), ALU.is_equal)

            dve.sem_inc(target_ready, 1)
            for c, w, u in each_unit(dve, g, "dve_unit"):
                if c is None:
                    continue
                G = dve.snap(u * GR)
                dve.wait_ge(target_ready, G + 1)
                nc.vector.tensor_copy(cur_hl[:, :], g.src_hl[:, bass.ds(c, 1), :].rearrange("p a t -> p (a t)"))
                src_c = g.srcF[:, bass.ds(c, 1), :].rearrange("p a t -> p (a t)")
                dst_c = g.dstF[:, bass.ds(c, 1), :].rearrange("p a t -> p (a t)")
                nc.vector.tensor_copy(cur_src[:, :], src_c)
                nc.vector.tensor_scalar(to_trash[:, :], src_c, -1.0, g.trash[:, 0:1], ALU.mult, ALU.add)
                nc.vector.tensor_scalar(cur_dst[:, :], dst_c, g.minB[:, bass.ds(c, 1)],
                                        g.win_off[:, bass.ds(w, 1)], ALU.subtract, ALU.subtract).then_inc(cur_ready, 1)
                dve.wait_ge(cur_ready, u + 1)
                one_hot(0)
                for j in range(GR):
                    t = slice(j * GT, (j + 1) * GT)
                    dve.wait_ge(spread_done, G + (j + 1))
                    nc.vector.tensor_tensor(eq[:, t, :], spread, bcast(cur_src[:, t], 2, P),
                                            ALU.is_equal).then_inc(eq_ready, 1)
                    if j + 1 < GR:
                        one_hot(j + 1)
                    dve.wait_ge(cnt_done, G + (j + 1))
                    nc.vector.scalar_tensor_tensor(out=moved[:, t], in0=ps_first[:, t], scalar=g.pow_lim[:, 0:1],
                                                   in1=to_trash[:, t], op0=ALU.is_gt, op1=ALU.mult).then_inc(mark_ready, 1)
                    dve.wait_ge(mark_ready, G + (j + 1))
                    dve.wait_ge(rows_free, G + (j + 1))
                    nc.vector.tensor_tensor(target[:, t], moved[:, t], cur_src[:, t], ALU.add).then_inc(target_ready, 1)

        @block.scalar
        def _(act):
            act.sem_inc(rows_ready, 1)
            for c, w, u in each_unit(act, g, "act_unit"):
                if c is None:
                    continue
                G = act.snap(u * GR)
                act.wait_ge(hl_turned, u + 1)
                nc.scalar.copy(src_rows[:, :], ps_hl[:, :]).then_inc(hl_copied, 1)
                for j in range(GR):
                    t = slice(j * GT, (j + 1) * GT)
                    act.wait_ge(cnt_done, G + (j + 1))
                    nc.scalar.copy(counts[:, :, :], cnt).then_inc(cnt_copied, 1)
                    act.wait_ge(sums_done, G + (j + 1 + GR))
                    act.wait_ge(rows_free, G + (j + 1))
                    nc.scalar.copy(rows[:, t, :], sums).then_inc(rows_ready, 1)

        @block.tensor
        def _(pe):
            def spread_group(j):
                for i in range(GT):
                    last = nc.tensor.matmul(spread[:, i, :], g.sel[:, j * GT + i, :], src_rows[:, :],
                                            start=True, stop=True)
                last.then_inc(spread_done, 1)

            pe.sem_inc(sums_done, GR)
            for c, w, u in each_unit(pe, g, "pe_unit"):
                if c is None:
                    continue
                G = pe.snap(u * GR)
                wait_alone(pe, cur_ready, u + 1, g.pe_turn)
                nc.tensor.transpose(ps_hl[:, :], cur_hl[:, :], g.identB[:, :]).then_inc(hl_turned, 1)
                pe.wait_ge(hl_copied, u + 1)
                spread_group(0)
                for j in range(GR):
                    pe.wait_ge(eq_ready, G + (j + 1))
                    for i in range(GT):
                        nc.tensor.matmul(cnt[:, i, :], oh[:, j * GT + i, :], eq[:, j * GT + i, :],
                                         start=True, stop=True)
                    for i in range(GT):
                        s = j * GT + i
                        last = nc.tensor.matmul(ps_first[:, s:s + 1], eq[:, s, :], g.pow_col[:, :],
                                                start=True, stop=True)
                    last.then_inc(cnt_done, 1)
                    if j + 1 < GR:
                        spread_group(j + 1)
                    pe.wait_ge(cnt_copied, G + (j + 1))
                    if j == 0:
                        pe.wait_ge(x_win_in, u * 16 + 16)
                    pe.wait_ge(rows_ready, G + (j + 1))
                    for i in range(GT):
                        for part in range(3):
                            last = nc.tensor.matmul(sums[:, i, :], counts[:, i, :], x_win[:, part, :],
                                                    start=(part == 0), stop=(part == 2))
                    last.then_inc(sums_done, 1)

        @block.gpsimd
        def _(pool):
            pool.sem_inc(rows_free, GR - 1)
            for c, w, u in each_unit(pool, g, "pool_unit"):
                G = pool.snap(u * GR)
                if c is None:
                    for k in range(ACCS):
                        pool.wait_ge(g.acc_done[k], G * 16 + 16)
                    continue
                for j in range(GR):
                    pool.wait_ge(rows_ready, G + (j + 2))
                    pool.wait_ge(target_ready, G + (j + 2))
                    before = pool.snap(G * 16 + 16 * (j + 1))
                    for i in range(GT):
                        s = j * GT + i
                        wait_alone(pool, g.acc_done[i], before, g.pool_turn)
                        pool.indirect_dma_start(g.acc[i][:, :], bass.IndirectOffsetOnAxis(target[:, s:s + 1], 0),
                                                rows[:, s, :], None, compute_op=ALU.add).then_inc(g.acc_done[i], 16)
                    pool.sem_inc(rows_free, 1)


def layer_norm(nc, dve, g, h, r, d, sq, stat, sems, n, out):
    mean_ready, centred, var_ready, std_ready, rstd_ready = sems
    nc.vector.tensor_reduce(stat[:, 0, :], r, AX_X, ALU.add).then_inc(mean_ready, 1)
    dve.wait_ge(mean_ready, n * 2 - 1)
    nc.vector.tensor_scalar_mul(stat[:, 1, :], stat[:, 0, :], 1.0 / g.D).then_inc(mean_ready, 1)
    dve.wait_ge(mean_ready, n * 2)
    nc.vector.tensor_tensor(d, r, bcast(stat[:, 1, :], 2, g.D), ALU.subtract).then_inc(centred, 1)
    dve.wait_ge(centred, n)
    nc.vector.tensor_tensor(sq, d, d, ALU.mult).then_inc(var_ready, 1)
    dve.wait_ge(var_ready, n * 3 - 2)
    nc.vector.tensor_reduce(stat[:, 2, :], sq, AX_X, ALU.add).then_inc(var_ready, 1)
    dve.wait_ge(var_ready, n * 3 - 1)
    nc.vector.tensor_scalar(stat[:, 3, :], stat[:, 2, :], 1.0 / g.D, EPS, ALU.mult, ALU.add).then_inc(var_ready, 1)
    dve.wait_ge(std_ready, n)
    nc.vector.reciprocal(stat[:, 5, :], stat[:, 4, :]).then_inc(rstd_ready, 1)
    dve.wait_ge(rstd_ready, n)
    return nc.vector.tensor_tensor(out, d, bcast(stat[:, 5, :], 2, g.D), ALU.mult)


def node_phase0(nc, g):
    C = BT * g.D
    H = BT * P // 2
    with ExitStack() as ctx:
        def sb(name, shape, dt=F32):
            return ctx.enter_context(nc.sbuf_tensor(name, shape, dt))

        def ps(name, shape):
            return ctx.enter_context(nc.psum_tensor(name, shape, F32))

        def sem(name):
            return ctx.enter_context(nc.semaphore(name))

        parts = sb("agg_in", [P, 2, ACCS, C])
        total = sb("total", [P, C])
        sT = sb("sT", [g.D, 2 * H])
        hT = sb("hT", [g.HID, 2, H])
        r = sb("r0", [P, BT, g.D])
        d = sb("d0", [P, BT, g.D])
        sq = sb("sq0", [P, BT, g.D])
        stat = sb("stat0", [P, 6, BT])
        x1 = sb("x1", [P, BT, g.D])
        x1T = sb("x1T", [g.D, 2 * H])
        nn = sb("nn", [P, 2, C])
        ps_s = ps("ps_s", [P, 2 * BANK])
        ps_h = ps("ps_h", [P, 2, BANK])
        ps_y = ps("ps_y", [P, BANK])
        ps_x = ps("ps_x", [P, 2 * BANK])
        ps_n = ps("ps_n", [P, BANK])

        agg_in = [sem(f"agg_in{h}") for h in range(2)]
        added = sem("added")
        s_turned = sem("s_turned")
        s_copied = sem("s_copied")
        h_done = sem("h_done")
        relu_done = sem("relu_done")
        y_done = sem("y_done")
        r_ready = sem("r_ready")
        ln_sems = [sem(f"ln0_{k}") for k in ("mean", "centred", "var", "std", "rstd")]
        x1_ready = sem("x1_ready")
        x1_turned = sem("x1_turned")
        x1_copied = sem("x1_copied")
        x1_kept = sem("x1_kept")
        nn_done = sem("nn_done")
        nn_copied = sem("nn_copied")
        nn_out = [sem(f"nn_out{h}") for h in range(2)]

        acc_v = [a[0:P * g.NT, :].rearrange("(p t) d -> p (t d)", t=g.NT) for a in g.acc]
        nn_v = g.nn[0:P * g.NT, :].rearrange("(p t) d -> p (t d)", t=g.NT)
        block = ctx.enter_context(nc.Block())

        @block.sync
        def _(sp):
            for h in range(2):
                for k in range(ACCS):
                    sp.dma_start(parts[:, h, k, :], acc_v[k][:, h * C:(h + 1) * C]).then_inc(agg_in[h], 16)
            with sp.Fori(0, g.NB // 2 - 1) as v:
                for h in range(2):
                    sp.wait_ge(added, (v * 2 + (h + 1)) * ACCS)
                    for k in range(ACCS):
                        sp.dma_start(parts[:, h, k, :], acc_v[k][:, bass.ds((v * 2 + (h + 2)) * C, C)]).then_inc(agg_in[h], 16)

        @block.vector
        def _(dve):
            dve.sem_inc(x1_ready, 1)
            with dve.Fori(0, g.NB // 2) as v:
                for h in range(2):
                    n = dve.snap(v * 2 + (h + 1))
                    col = dve.snap((v * 2 + h) * C)
                    x = g.xres[:, bass.ds(col, C)]
                    dve.wait_ge(agg_in[h], (v + 1) * (16 * ACCS))
                    for k in range(ACCS):
                        if k == 0:
                            ins = nc.vector.tensor_tensor(total[:, :], x, parts[:, h, 0, :], ALU.add)
                        else:
                            dve.wait_ge(added, n * ACCS - (ACCS - k))
                            ins = nc.vector.tensor_tensor(total[:, :], total[:, :], parts[:, h, k, :], ALU.add)
                        ins.then_inc(added, 1)
                    dve.wait_ge(y_done, n)
                    dve.wait_ge(x1_ready, n)
                    nc.vector.tensor_tensor(r[:, :, :].rearrange("p t d -> p (t d)"), ps_y[:, 0:C], x,
                                            ALU.add).then_inc(r_ready, 1)
                    dve.wait_ge(r_ready, n)
                    layer_norm(nc, dve, g, h, r[:, :, :], d[:, :, :], sq[:, :, :], stat, ln_sems, n,
                               x1[:, :, :]).then_inc(x1_ready, 1)

        @block.scalar
        def _(act):
            for h in range(2):
                act.sem_inc(nn_out[h], 16)
            with act.Fori(0, g.NB // 2) as v:
                for h in range(2):
                    n = act.snap(v * 2 + (h + 1))
                    col = act.snap((v * 2 + h) * C)
                    act.wait_ge(s_turned, n)
                    nc.scalar.copy(sT[:, :], ps_s[0:g.D, 0:2 * H]).then_inc(s_copied, 1)
                    act.wait_ge(h_done, n)
                    nc.scalar.activation(hT[:, :, :], ps_h[:, :, 0:H], ACT.Relu, bias=g.b1[:, 0:1]).then_inc(relu_done, 1)
                    act.wait_ge(ln_sems[2], n * 3)
                    nc.scalar.sqrt(stat[:, 4, :], stat[:, 3, :]).then_inc(ln_sems[3], 1)
                    act.wait_ge(x1_ready, n + 1)
                    nc.scalar.copy(g.xres[:, bass.ds(col, C)], x1[:, :, :].rearrange("p t d -> p (t d)")).then_inc(x1_kept, 1)
                    act.wait_ge(x1_turned, n)
                    nc.scalar.copy(x1T[:, :], ps_x[0:g.D, 0:2 * H]).then_inc(x1_copied, 1)
                    act.wait_ge(nn_done, n)
                    act.wait_ge(nn_out[h], (v + 1) * 16)
                    nc.scalar.copy(nn[:, h, :], ps_n[:, 0:C]).then_inc(nn_copied, 1)
                    act.wait_ge(nn_copied, n)
                    act.dma_start(nn_v[:, bass.ds(col, C)], nn[:, h, :]).then_inc(nn_out[h], 16)
            for h in range(2):
                act.wait_ge(nn_out[h], 16 * (g.NB // 2 + 1))

        @block.tensor
        def _(pe):
            with pe.Fori(0, g.NB // 2) as v:
                for h in range(2):
                    n = pe.snap(v * 2 + (h + 1))
                    wait_alone(pe, added, n * ACCS, g.pe_turn)
                    for t in range(BT):
                        last = nc.tensor.transpose(ps_s[0:g.D, t * P:(t + 1) * P], total[:, t * g.D:(t + 1) * g.D], g.identF[:, :])
                    last.then_inc(s_turned, 1)
                    pe.wait_ge(s_copied, n)
                    for k in range(2):
                        last = nc.tensor.matmul(ps_h[:, k, 0:H], g.W1[:, :], sT[:, k * H:(k + 1) * H], start=True, stop=True)
                    last.then_inc(h_done, 1)
                    pe.wait_ge(relu_done, n)
                    nc.tensor.matmul(ps_y[:, 0:C], g.ones[:, :], g.b2rep[:, :, :].rearrange("o t d -> o (t d)"),
                                     start=True, stop=False, skip_group_check=True)
                    hv = hT[:, :, :].rearrange("p a b -> p (a b)")
                    for t in range(BT):
                        last = nc.tensor.matmul(ps_y[:, t * g.D:(t + 1) * g.D], hv[:, t * P:(t + 1) * P], g.W2[:, :],
                                                start=False, stop=(t == BT - 1), skip_group_check=True)
                    last.then_inc(y_done, 1)
                    wait_alone(pe, x1_ready, n + 1, g.pe_turn)
                    for t in range(BT):
                        last = nc.tensor.transpose(ps_x[0:g.D, t * P:(t + 1) * P], x1[:, t, :], g.identF[:, :])
                    last.then_inc(x1_turned, 1)
                    pe.wait_ge(x1_copied, n)
                    for t in range(BT):
                        last = nc.tensor.matmul(ps_n[:, t * g.D:(t + 1) * g.D], x1T[:, t * P:(t + 1) * P], g.V1T[:, :],
                                                start=True, stop=True)
                    last.then_inc(nn_done, 1)


def layer1_edges(nc, g):
    HALF = GT * P // 2
    MID = GT // 2
    ZB = 3
    with ExitStack() as ctx:
        def sb(name, shape, dt=F32):
            return ctx.enter_context(nc.sbuf_tensor(name, shape, dt))

        def ps(name, shape):
            return ctx.enter_context(nc.psum_tensor(name, shape, F32))

        def sem(name):
            return ctx.enter_context(nc.semaphore(name))

        ea = sb("ea", [P, CT, g.F])
        ea_T = sb("ea_T", [g.F, 2, HALF])
        cur_dst = sb("cur_dst1", [P, CT])
        oh = sb("oh1", [P, CT, WIN])
        y_cap = sb("y_cap", [P, HALF])
        e_y = sb("e_y", [P, HALF])
        q = sb("q", [P, HALF])
        sp_y = sb("sp_y", [P, GR, HALF])
        idx = sb("idx", [P, CT], I32)
        nn = sb("nn_rows", [P, CT, g.D])
        msg = sb("msg", [P, CT, g.D])
        seg = sb("seg", [WIN, g.D])
        cf_old = sb("cf_old", [WIN, g.D])
        ps_t = ps("ps_t", [P, 2, BANK])
        ps_z = ps("ps_z", [P, ZB, BANK])
        ps_e = ps("ps_e", [P, 2, BANK])
        ps_seg = ps("ps_seg", [P, BANK])

        ea_in = [sem(f"ea_in{j}") for j in range(GR)]
        idx_in = [sem(f"idx_in{j}") for j in range(GR)]
        gathered = [sem(f"gathered{j}") for j in range(GR)]
        turned = sem("turned")
        turn_copied = sem("turn_copied")
        z_done = sem("z_done")
        capped = sem("capped")
        exp_done = sem("exp_done")
        log_done = sem("log_done")
        sp_ready = sem("sp_ready")
        h_done = sem("h_done1")
        msg_ready = sem("msg_ready")
        dst_ready = sem("dst_ready")
        seg_group = sem("seg_group")
        seg_ready = sem("seg_ready")
        cf_in = sem("cf_old_in")
        cf_out = sem("cf_out")

        src_v = g.ins["src"].rearrange("(c p t) -> p c t", p=P, t=CT)
        ea_v = g.ins["edge_attr_128"].rearrange("(c p t) f -> c p (t f)", p=P, t=CT)
        block = ctx.enter_context(nc.Block())

        @block.sync
        def _(sp):
            def load_attributes(c, j, G):
                sp.wait_ge(turned, G + (j + 1))
                sp.dma_start(ea[:, j * GT:(j + 1) * GT, :].rearrange("p t f -> p (t f)"),
                             ea_v[bass.ds(c, 1), :, j * GT * g.F:(j + 1) * GT * g.F].rearrange("a p f -> (a p) f")
                             ).then_inc(ea_in[j], 16)

            last_base = sp.alloc_register("last_base")
            sp.reg_mov(last_base, 0)

            def store_window(u):
                sp.wait_ge(seg_ready, u + 1)
                last = sp.snap(last_base, min_val=0, max_val=g.N - 1)
                sp.dma_start(g.cf[bass.ds(last, WIN), :], seg[:, :]).then_inc(cf_out, 16)
                wait_alone(sp, cf_out, u * 16 + 16, g.sp_turn)

            for c, w, u in each_unit(sp, g, "sp_unit1"):
                G = sp.snap(u * GR)
                if c is None:
                    for j in range(2):
                        load_attributes(0, j, G)
                    store_window(u)
                    continue
                base = window_base(sp, g, c, w, "sp_base1")
                for j in range(GR):
                    load_attributes(c, j, G)
                    sp.wait_ge(msg_ready, G + (j + 1))
                    with nc.allow_non_contiguous_dma("five indices a partition"):
                        sp.dma_start(idx[:, j * GT:(j + 1) * GT],
                                     src_v[:, bass.ds(c, 1), j * GT:(j + 1) * GT].rearrange("p a t -> p (a t)")
                                     ).then_inc(idx_in[j], 16)
                store_window(u)
                sp.dma_start(cf_old[:, :], g.cf[bass.ds(base, WIN), :]).then_inc(cf_in, 16)
                sp.reg_mov(last_base, base)

        @block.gpsimd
        def _(pool):
            for c, w, u in each_unit(pool, g, "pool_unit1"):
                if c is None:
                    continue
                G = pool.snap(u * GR)
                for j in range(GR):
                    pool.wait_ge(idx_in[j], u * 16 + 16)
                    wait_alone(pool, msg_ready, G + (j + 1), g.pool_turn)
                    for i in range(GT):
                        s = j * GT + i
                        pool.indirect_dma_start(nn[:, s, :], None, g.nn[0:g.N, :],
                                                bass.IndirectOffsetOnAxis(idx[:, s:s + 1], 0)).then_inc(gathered[j], 16)

        @block.vector
        def _(dve):
            def message(j, G, u):
                t = slice(j * GT, (j + 1) * GT)
                dve.wait_ge(h_done, G + (j + 1))
                dve.wait_ge(gathered[j], u * (16 * GT) + 16 * GT)
                nc.vector.tensor_tensor(msg[:, t, :], ps_e[:, j % 2, 0:GT * g.D].rearrange("p (t d) -> p t d", d=g.D),
                                        nn[:, t, :], ALU.mult).then_inc(msg_ready, 1)

            def cap(j, G):
                dve.wait_ge(z_done, G + (j + 1))
                nc.vector.tensor_scalar(y_cap[:, :], ps_z[:, j % GR % ZB, 0:HALF], g.bc1h[:, 0:1], CAP,
                                        ALU.add, ALU.min).then_inc(capped, 1)

            def softplus(j, G):
                dve.wait_ge(log_done, G + (j + 1))
                nc.vector.scalar_tensor_tensor(out=sp_y[:, j % GR, :], in0=ps_z[:, j % GR % ZB, 0:HALF],
                                               scalar=g.bc1h[:, 0:1], in1=q[:, :],
                                               op0=ALU.add, op1=ALU.max).then_inc(sp_ready, 1)

            dve.sem_inc(msg_ready, GR)
            nc.vector.memset(seg[:, :], 0.0).then_inc(seg_ready, 1)
            cap(0, 0)
            softplus(0, 0)
            for c, w, u in each_unit(dve, g, "dve_unit1"):
                if c is None:
                    continue
                G = dve.snap(u * GR)
                dst_c = g.dstF[:, bass.ds(c, 1), :].rearrange("p a t -> p (a t)")
                dve.wait_ge(msg_ready, G + GR)
                nc.vector.tensor_scalar(cur_dst[:, :], dst_c, g.minB[:, bass.ds(c, 1)],
                                        g.win_off[:, bass.ds(w, 1)], ALU.subtract, ALU.subtract).then_inc(dst_ready, 1)
                for j in range(GR):
                    t = slice(j * GT, (j + 1) * GT)
                    cap(j + 1, G)
                    if j == 0:
                        dve.wait_ge(dst_ready, u + 1)
                    dve.wait_ge(seg_group, G + (j + 1))
                    nc.vector.tensor_tensor(oh[:, t, :], bcast(g.iota_w[:, :], 1, GT),
                                            bcast(cur_dst[:, t], 2, WIN), ALU.is_equal)
                    if j > 0:
                        message(j - 1, G, u)
                    softplus(j + 1, G)
                message(GR - 1, G, u)
                dve.wait_ge(seg_group, G + 2 * GR)
                dve.wait_ge(cf_in, u * 16 + 16)
                nc.vector.tensor_tensor(seg[:, :], ps_seg[:, 0:g.D], cf_old[:, :], ALU.add).then_inc(seg_ready, 1)

        @block.scalar
        def _(act):
            def copy_turned(j, G):
                act.wait_ge(turned, G + (j + 1 + GR))
                nc.scalar.copy(ea_T[:, :, :], ps_t[:, :, 0:HALF]).then_inc(turn_copied, 1)

            def logarithm(j, G):
                act.wait_ge(capped, G + (j + 1))
                nc.scalar.activation(e_y[:, :], y_cap[:, :], ACT.Exp).then_inc(exp_done, 1)
                act.wait_ge(exp_done, G + (j + 1))
                nc.scalar.activation(q[:, :], e_y[:, :], ACT.Ln, bias=1.0).then_inc(log_done, 1)

            act.preload_act_table_set("natural_log_exp_and_others")
            copy_turned(0, 0)
            logarithm(0, 0)
            copy_turned(1, 0)
            for c, w, u in each_unit(act, g, "act_unit1"):
                if c is None:
                    continue
                G = act.snap(u * GR)
                for j in range(GR):
                    logarithm(j + 1, G)
                    copy_turned(j + 2, G)

        @block.tensor
        def _(pe):
            def turn(j, G, rounds):
                pe.wait_ge(ea_in[j % GR], rounds)
                for bank, at, i in ((1, HALF - P, MID), (0, 0, 0), (0, P, 1), (0, 2 * P, MID), (1, 0, 3), (1, P, 4)):
                    last = nc.tensor.transpose(ps_t[:, bank, at:at + P], ea[:, j % GR * GT + i, :], g.identF[:, :])
                last.then_inc(turned, 1)

            def first(j, G):
                pe.wait_ge(turn_copied, G + (j + 1))
                z = ps_z[:, j % GR % ZB, 0:HALF]
                nc.tensor.matmul(z[0:g.D, :], g.Wc1T[:, :], ea_T[:, 0, :], start=True, stop=True)
                nc.tensor.matmul(z[g.D:P, :], g.Wc1T[:, :], ea_T[:, 1, :], start=True, stop=True).then_inc(z_done, 1)

            def second(j, G):
                pe.wait_ge(sp_ready, G + (j + 1))
                out = ps_e[:, j % 2, 0:GT * g.D]
                nc.tensor.matmul(out, g.ones3[:, :], g.bc2p[:, :, :].rearrange("o t d -> o (t d)"),
                                 start=True, stop=False, skip_group_check=True)
                tiles = out.rearrange("p (t d) -> p t d", d=g.D)
                for i in range(MID):
                    nc.tensor.matmul(tiles[:, i:GT:MID + 1, :], sp_y[:, j, i * P:(i + 1) * P], g.Wc2d[:, :, :],
                                     start=False, stop=False, skip_group_check=True)
                for k in range(2):
                    last = nc.tensor.matmul(tiles[k * g.D:(k + 1) * g.D, MID, :], sp_y[:, j, MID * P:HALF],
                                            g.Wc2d[:, k, :], start=False, stop=True, skip_group_check=True)
                last.then_inc(h_done, 1)

            def sum_up(j, G, u):
                pe.wait_ge(msg_ready, G + (j + 1 + GR))
                if j == 0:
                    pe.wait_ge(seg_ready, u + 1)
                for i in range(GT):
                    s = j * GT + i
                    last = nc.tensor.matmul(ps_seg[:, 0:g.D], oh[:, s, :], msg[:, s, :],
                                            start=(s == 0), stop=(s == CT - 1))
                last.then_inc(seg_group, 1)

            pe.sem_inc(turned, GR)
            pe.sem_inc(seg_group, GR)
            turn(0, 0, 16)
            first(0, 0)
            turn(1, 0, 16)
            for c, w, u in each_unit(pe, g, "pe_unit1"):
                if c is None:
                    continue
                G = pe.snap(u * GR)
                for j in range(GR):
                    first(j + 1, G)
                    if j + 2 < GR:
                        turn(j + 2, G, u * 16 + 16)
                    else:
                        turn(j + 2, G, u * 16 + 32)
                    if j > 0:
                        sum_up(j - 1, G, u)
                    second(j, G)
                sum_up(GR - 1, G, u)


def node_phase1(nc, g):
    C = BT * g.D
    H = BT * P // 2
    with ExitStack() as ctx:
        def sb(name, shape, dt=F32):
            return ctx.enter_context(nc.sbuf_tensor(name, shape, dt))

        def ps(name, shape):
            return ctx.enter_context(nc.psum_tensor(name, shape, F32))

        def sem(name):
            return ctx.enter_context(nc.semaphore(name))

        cf = sb("cf_in_sb", [P, 2, C])
        cT = sb("cT", [g.D, 2 * H])
        y_cap = sb("y_cap1", [g.D, 2, H])
        e_y = sb("e_y1", [g.D, 2, H])
        q = sb("q1", [g.D, 2, H])
        sp_y = sb("sp_y1", [g.D, 2, H])
        r = sb("r1", [P, BT, g.D])
        d = sb("d1", [P, BT, g.D])
        sq = sb("sq1", [P, BT, g.D])
        stat = sb("stat1", [P, 6, BT])
        ps_c = ps("ps_c", [P, 2 * BANK])
        ps_z = ps("ps_z1", [g.D, 2, BANK])
        ps_y = ps("ps_y1", [P, BANK])

        cf_in = [sem(f"cf_in{h}") for h in range(2)]
        c_turned = sem("c_turned")
        c_copied = sem("c_copied")
        z_done = sem("z_done2")
        capped = sem("capped2")
        exp_done = sem("exp_done2")
        log_done = sem("log_done2")
        sp_ready = sem("sp_ready2")
        y_done = sem("y_done2")
        r_ready = sem("r_ready2")
        ln_sems = [sem(f"ln1_{k}") for k in ("mean", "centred", "var", "std", "rstd")]
        out_ready = sem("out_ready")
        stored = sem("stored")

        cf_v = g.cf[0:P * g.NT, :].rearrange("(p t) d -> p (t d)", t=g.NT)
        block = ctx.enter_context(nc.Block())

        @block.sync
        def _(sp):
            for h in range(2):
                sp.dma_start(cf[:, h, :], cf_v[:, h * C:(h + 1) * C]).then_inc(cf_in[h], 16)
            with sp.Fori(0, g.NB // 2 - 1) as v:
                for h in range(2):
                    sp.wait_ge(c_turned, v * 2 + (h + 1))
                    sp.dma_start(cf[:, h, :], cf_v[:, bass.ds((v * 2 + (h + 2)) * C, C)]).then_inc(cf_in[h], 16)
            sp.wait_ge(out_ready, g.NB + 1)
            load_nodes(sp, g, g.xres, g.out, stored, store=True)
            sp.wait_ge(stored, 48)

        @block.tensor
        def _(pe):
            with pe.Fori(0, g.NB // 2) as v:
                for h in range(2):
                    n = pe.snap(v * 2 + (h + 1))
                    wait_alone(pe, cf_in[h], v * 16 + 16, g.pe_turn)
                    for t in range(BT):
                        last = nc.tensor.transpose(ps_c[0:g.D, t * P:(t + 1) * P], cf[:, h, t * g.D:(t + 1) * g.D], g.identF[:, :])
                    last.then_inc(c_turned, 1)
                    wait_alone(pe, c_copied, n, g.pe_turn)
                    for k in range(2):
                        last = nc.tensor.matmul(ps_z[:, k, 0:H], g.V2T[:, :], cT[:, k * H:(k + 1) * H], start=True, stop=True)
                    last.then_inc(z_done, 1)
                    nc.tensor.matmul(ps_y[:, 0:C], g.ones[:, :], g.v3rep[:, :, :].rearrange("o t d -> o (t d)"),
                                     start=True, stop=False, skip_group_check=True)
                    pe.wait_ge(sp_ready, n)
                    sv = sp_y[:, :, :].rearrange("p a b -> p (a b)")
                    for t in range(BT):
                        last = nc.tensor.matmul(ps_y[:, t * g.D:(t + 1) * g.D], sv[:, t * P:(t + 1) * P], g.V3T[:, :],
                                                start=False, stop=(t == BT - 1), skip_group_check=True)
                    last.then_inc(y_done, 1)

        @block.scalar
        def _(act):
            with act.Fori(0, g.NB // 2) as v:
                for h in range(2):
                    n = act.snap(v * 2 + (h + 1))
                    act.wait_ge(c_turned, n)
                    nc.scalar.copy(cT[:, :], ps_c[0:g.D, 0:2 * H]).then_inc(c_copied, 1)
                    act.wait_ge(capped, n)
                    nc.scalar.activation(e_y[:, :, :], y_cap[:, :, :], ACT.Exp).then_inc(exp_done, 1)
                    act.wait_ge(exp_done, n)
                    nc.scalar.activation(q[:, :, :], e_y[:, :, :], ACT.Ln, bias=1.0).then_inc(log_done, 1)
                    act.wait_ge(ln_sems[2], n * 3)
                    nc.scalar.sqrt(stat[:, 4, :], stat[:, 3, :]).then_inc(ln_sems[3], 1)

        @block.vector
        def _(dve):
            dve.sem_inc(out_ready, 1)
            with dve.Fori(0, g.NB // 2) as v:
                for h in range(2):
                    n = dve.snap(v * 2 + (h + 1))
                    col = dve.snap((v * 2 + h) * C)
                    x = g.xres[:, bass.ds(col, C)]
                    dve.wait_ge(z_done, n)
                    nc.vector.tensor_scalar(y_cap[:, :, :], ps_z[:, :, 0:H], g.v2h[:, 0:1], CAP,
                                            ALU.add, ALU.min).then_inc(capped, 1)
                    dve.wait_ge(log_done, n)
                    nc.vector.scalar_tensor_tensor(out=sp_y[:, :, :], in0=ps_z[:, :, 0:H], scalar=g.v2h[:, 0:1],
                                                   in1=q[:, :, :], op0=ALU.add, op1=ALU.max).then_inc(sp_ready, 1)
                    dve.wait_ge(y_done, n)
                    dve.wait_ge(out_ready, n)
                    nc.vector.scalar_tensor_tensor(out=r[:, :, :].rearrange("p t d -> p (t d)"), in0=x, scalar=2.0,
                                                   in1=ps_y[:, 0:C], op0=ALU.mult, op1=ALU.add).then_inc(r_ready, 1)
                    dve.wait_ge(r_ready, n)
                    layer_norm(nc, dve, g, h, r[:, :, :], d[:, :, :], sq[:, :, :], stat, ln_sems, n,
                               x.rearrange("p (t d) -> p t d", d=g.D)).then_inc(out_ready, 1)


def build(nc, ins, out):
    with ExitStack() as ctx:
        g = make_plan(nc, ctx, ins, out)
        prep_phase(nc, g)
        layer0_edges(nc, g)
        node_phase0(nc, g)
        layer1_edges(nc, g)
        node_phase1(nc, g)


_INS = ["x", "src", "dst", "edge_attr_128", "L0_gnn_W1", "L0_gnn_b1", "L0_gnn_W2", "L0_gnn_b2", "L1_gnn_W1",
        "L1_gnn_Wc1", "L1_gnn_bc1", "L1_gnn_Wc2", "L1_gnn_bc2", "L1_gnn_W2", "L1_gnn_b2", "L1_gnn_W3", "L1_gnn_b3"]


def kernel(**inputs):
    import numpy as _np
    import concourse.bacc as _bacc
    from concourse import mybir as _mybir
    from concourse.bass_utils import run_bass_kernel_spmd as _run

    nc = _bacc.Bacc("TRN2", target_bir_lowering=False, num_devices=1)
    arrays, aps = {}, {}
    for name in _INS:
        a = _np.ascontiguousarray(inputs[name])
        arrays[f"in_{name}_dram"] = a
        aps[name] = nc.dram_tensor(f"in_{name}_dram", a.shape, _mybir.dt.from_np(a.dtype), kind="ExternalInput").ap()
    out = nc.dram_tensor("out_0_dram", inputs["x"].shape, _mybir.dt.float32, kind="ExternalOutput").ap()
    build(nc, aps, out)
    r = _run(nc, [arrays], core_ids=[0])
    return r.results[0]["out_0_dram"]
```

```python
from contextlib import ExitStack

import concourse.bass as bass
from concourse import mybir

F32 = mybir.dt.float32
BF16 = mybir.dt.bfloat16
I32 = mybir.dt.int32
ALU = mybir.AluOpType
ACT = mybir.ActivationFunctionType
AX_X = mybir.AxisListType.X

P = 128
GT = 5
GR = 5
CT = GT * GR
WIN = 128
ACCS = 5
BT = 7
EPS = 1e-5
CAP = 20.0
BANK = 512


def bcast(ap, axis, n):
    shape = list(ap.shape)
    return ap.unsqueeze(axis).broadcast_to(shape[:axis] + [n] + shape[axis:])


def wait_alone(eng, sem, value, turn):
    eng.wait_ge(sem, value)
    eng.sem_inc(turn, 1)


def held(eng, value):
    return value if isinstance(value, int) else eng.snap(value)


def split_steps(nc, part, left, value):
    return (lambda: nc.vector.tensor_copy(part[0], value),
            lambda: nc.vector.tensor_tensor(left[0], value, part[0], ALU.subtract),
            lambda: nc.vector.tensor_copy(part[1], left[0]),
            lambda: nc.vector.tensor_tensor(left[1], left[0], part[1], ALU.subtract),
            lambda: nc.vector.tensor_copy(part[2], left[1]))


SPLIT = 5


class Plan:
    pass


def make_plan(nc, ctx, ins, out):
    g = Plan()
    g.ins, g.out = ins, out
    g.N, g.D = ins["x"].shape
    g.E, g.F = ins["edge_attr_128"].shape
    g.HID = ins["L0_gnn_W1"].shape[1]
    g.NC = g.E // (P * CT)
    g.NT = -(-g.N // P)
    g.NB = g.NT // BT
    g.NW = -(-g.N // WIN)
    g.ROWS = P * (g.NT + 1)
    assert g.E == g.NC * P * CT and g.NT == g.NB * BT and g.NB % 2 == 0
    assert g.ROWS >= g.N + P and g.ROWS >= g.N + WIN and g.D == 64 and g.F == P and g.HID == P
    assert g.NC <= P

    def dram(name, cols, dt):
        return nc.dram_tensor(name, (g.ROWS, cols), dt, kind="Internal").ap()

    g.acc = [dram(f"agg_part{k}", g.D, F32) for k in range(ACCS)]
    g.cf = dram("cf_node", g.D, F32)
    g.nn = dram("new_node", g.D, F32)
    g.xp = dram("x_padded", g.D, F32)

    def sb(name, shape, dt):
        return ctx.enter_context(nc.sbuf_tensor(name, shape, dt))

    g.identF = sb("identF", [P, P], F32)
    g.identB = sb("identB", [P, P], BF16)
    g.iota_w = sb("iota_w", [P, WIN], F32)
    g.win_off = sb("win_off", [P, g.NW], F32)
    g.pow_col = sb("pow_col", [P, 1], BF16)
    g.pow_lim = sb("pow_lim", [P, 1], F32)
    g.trash = sb("trash", [P, 1], F32)
    g.sel = sb("sel", [2 * CT, CT, P], BF16)
    g.srcF = sb("srcF", [P, g.NC, CT], F32)
    g.dstF = sb("dstF", [P, g.NC, CT], F32)
    g.src_hl = sb("src_hl", [P, g.NC, 2 * CT], BF16)
    g.minB = sb("minB", [P, g.NC], F32)
    g.tab_min = sb("tab_min", [P, g.NC], I32)
    g.tab_nw = sb("tab_nw", [P, g.NC], I32)
    g.zeros = sb("zeros", [P, g.ROWS // P * g.D], F32)
    g.xres = sb("xres", [P, g.NT * g.D], F32)
    g.W1 = sb("W1", [g.D, g.HID], F32)
    g.b1 = sb("b1", [g.HID, 1], F32)
    g.W2 = sb("W2", [g.HID, g.D], F32)
    g.b2p = sb("b2p", [3, BT, g.D], BF16)
    g.V1T = sb("V1T", [g.D, g.D], F32)
    g.Wc1T = sb("Wc1T", [g.F, g.D], F32)
    g.bc1h = sb("bc1h", [P, 1], F32)
    g.Wc2d = sb("Wc2d", [P, 2, g.D], F32)
    g.bc2p = sb("bc2p", [3, GT, g.D], BF16)
    g.ones3 = sb("ones3", [3, P], BF16)
    g.V2T = sb("V2T", [g.D, g.D], F32)
    g.v2h = sb("v2h", [g.D, 1], F32)
    g.V3T = sb("V3T", [g.D, g.D], F32)
    g.v3p = sb("v3p", [3, BT, g.D], BF16)
    g.acc_done = [ctx.enter_context(nc.semaphore(f"acc_done{k}")) for k in range(ACCS)]
    g.pool_turn = ctx.enter_context(nc.semaphore("pool_turn"))
    g.sp_turn = ctx.enter_context(nc.semaphore("sp_turn"))
    g.pe_turn = ctx.enter_context(nc.semaphore("pe_turn"))
    return g


def load_nodes(eng, g, tile, dram, sem):
    row = g.NT * g.D
    full = g.N // g.NT
    even = full // 16 * 16
    rest = (g.N - full * g.NT) * g.D
    whole = dram[0:full * g.NT, :].rearrange("(p t) d -> p (t d)", t=g.NT)
    last = dram[full * g.NT:g.N, :].rearrange("(o t) d -> o (t d)", o=1)
    for s, d in ((tile[0:even, :], whole[0:even, :]), (tile[even:full, :], whole[even:full, :]),
                 (tile[full:full + 1, 0:rest], last)):
        eng.dma_start(s, d).then_inc(sem, 16)
    assert full + 1 == P and row == tile.shape[1]


def prep_phase(nc, g):
    ins = g.ins
    with ExitStack() as ctx:
        def sb(name, shape, dt):
            return ctx.enter_context(nc.sbuf_tensor(name, shape, dt))

        def sem(name):
            return ctx.enter_context(nc.semaphore(name))

        idx_i = sb("idx_i", [P, 2, g.NC, CT], I32)
        digit = sb("digit", [P, g.NC, CT], I32)
        int_c = sb("int_c", [P, WIN + g.NW + 3], I32)
        wload = sb("wload", [g.D, 5, P], F32)
        ext = sb("ext", [P, 2, g.NC], F32)
        colx = sb("colx", [P, 2], F32)
        colb = sb("colb", [P, 2, P], F32)
        bias = sb("bias", [1, 3, g.D], F32)
        bias_part = sb("bias_part", [1, 3, 3, g.D], BF16)
        bias_left = sb("bias_left", [1, 2, 3, g.D], F32)
        ps_t = ctx.enter_context(nc.psum_tensor("prep_t", [P, 2, BANK], F32))
        ps_w = ctx.enter_context(nc.psum_tensor("prep_w", [P, 5, P], F32))

        src_in = sem("src_in")
        dst_in = sem("dst_in")
        w_in = sem("w_in")
        zeroed = sem("zeroed")
        const_set = sem("const_set")
        const_sel = sem("const_sel")
        iota_done = sem("iota_done")
        v_step = sem("v_step")
        ext_ready = sem("ext_ready")
        ext_turned = sem("ext_turned")
        col_ready = sem("col_ready")
        ext_spread = sem("ext_spread")
        w_turned = sem("w_turned")
        xp_out = sem("xp_out")
        digit_ready = sem("digit_ready")
        bias_split = sem("bias_split")
        bias_in = sem("bias_in")
        bias_spread = sem("bias_spread")

        src_v = ins["src"].rearrange("(c p t) -> p c t", p=P, t=CT)
        dst_v = ins["dst"].rearrange("(c p t) -> p c t", p=P, t=CT)

        def flat(nodes):
            return nodes.rearrange("n d -> (n d)").rearrange("(a b) -> a b", a=10 * 16)

        block = ctx.enter_context(nc.Block())

        @block.sync
        def _(sp):
            sp.dma_start(idx_i[:, 1, :, :], dst_v).then_inc(dst_in, 16)
            sp.dma_start(idx_i[:, 0, :, :], src_v).then_inc(src_in, 16)
            sp.dma_start(flat(g.xp[0:g.N, :]), flat(ins["x"])).then_inc(xp_out, 16)
            sp.wait_ge(zeroed, 1)
            sp.dma_start(g.xp[g.N:g.N + P, :], g.zeros[:, 0:g.D]).then_inc(xp_out, 16)
            sp.dma_start(g.xp[g.N + P:g.ROWS, :], g.zeros[0:g.ROWS - g.N - P, 0:g.D]).then_inc(xp_out, 16)
            sp.dma_start(g.acc[0][g.N:g.N + P, :], g.zeros[:, 0:g.D]).then_inc(xp_out, 16)
            sp.dma_start(g.acc[0][g.N + P:g.ROWS, :], g.zeros[0:g.ROWS - g.N - P, 0:g.D]).then_inc(xp_out, 16)
            sp.wait_ge(xp_out, 80)

        @block.scalar
        def _(act):
            def small(out, in_):
                act.dma_start(out, in_).then_inc(w_in, 16)

            def column(v):
                return v.rearrange("(n o) -> n o", o=1)

            def row(v):
                return v.rearrange("(o n) -> o n", o=1)

            for k, name in enumerate(("L0_gnn_b2", "L1_gnn_bc2", "L1_gnn_b3")):
                act.dma_start(bias[:, k, :], row(ins[name])).then_inc(bias_in, 16)
            small(g.W1[:, :], ins["L0_gnn_W1"])
            small(g.W2[:, :], ins["L0_gnn_W2"])
            small(g.b1[:, :], column(ins["L0_gnn_b1"]))
            small(wload[:, 0, 0:g.D], ins["L1_gnn_W1"])
            small(wload[:, 1, :], ins["L1_gnn_Wc1"])
            small(wload[:, 2, 0:g.D], ins["L1_gnn_Wc2"])
            small(wload[:, 2, g.D:P], ins["L1_gnn_Wc2"])
            small(wload[:, 3, 0:g.D], ins["L1_gnn_W2"])
            small(wload[:, 4, 0:g.D], ins["L1_gnn_W3"])
            small(g.bc1h[0:g.D, :], column(ins["L1_gnn_bc1"]))
            small(g.bc1h[g.D:P, :], column(ins["L1_gnn_bc1"]))
            small(g.v2h[:, :], column(ins["L1_gnn_b2"]))
            act.wait_ge(src_in, 16)
            nc.scalar.copy(g.srcF[:, :, :], idx_i[:, 0, :, :])
            act.wait_ge(digit_ready, 1)
            nc.scalar.copy(g.src_hl[:, :, 0:CT], idx_i[:, 1, :, :])
            act.wait_ge(digit_ready, 2)
            nc.scalar.copy(g.src_hl[:, :, CT:2 * CT], digit[:, :, :])
            act.wait_ge(bias_split, 1)
            for k, (to, n) in enumerate(((g.b2p, BT), (g.bc2p, GT), (g.v3p, BT))):
                for part in range(3):
                    act.dma_start(to[part:part + 1, :, :], bcast(bias_part[:, part, k, :], 1, n)).then_inc(bias_spread, 16)
            act.wait_ge(bias_spread, 16 * 9)

        @block.gpsimd
        def _(pool):
            nc.gpsimd.memset(g.zeros[:, :], 0.0).then_inc(zeroed, 1)
            nc.gpsimd.memset(g.identF[:, :], 0.0).then_inc(const_set, 1)
            nc.gpsimd.memset(g.identB[:, :], 0.0).then_inc(const_set, 1)
            nc.gpsimd.memset(g.sel[:, :, :], 0.0).then_inc(const_set, 1)
            nc.gpsimd.memset(g.ones3[:, :], 1.0).then_inc(const_set, 1)
            o = WIN + g.NW
            nc.gpsimd.iota(int_c[:, 0:WIN], [[1, WIN]], 0, 0).then_inc(iota_done, 1)
            nc.gpsimd.iota(int_c[:, WIN:o], [[WIN, g.NW]], 0, 0).then_inc(iota_done, 1)
            nc.gpsimd.iota(int_c[:, o:o + 1], [[0, 1]], g.N, 1).then_inc(iota_done, 1)
            nc.gpsimd.iota(int_c[:, o + 1:o + 2], [[0, 1]], (127 + 63) << 23, -(1 << 23)).then_inc(iota_done, 1)
            nc.gpsimd.iota(int_c[:, o + 2:o + 3], [[0, 1]], ((127 + 64) << 23) + (1 << 21), -(1 << 23)).then_inc(iota_done, 1)
            pool.wait_ge(zeroed, 1)
            pool.dma_start(flat(g.acc[0][0:g.N, :]), flat(ins["x"])).then_inc(g.acc_done[0], 16)
            for k in range(1, ACCS):
                pool.dma_start(g.acc[k].rearrange("(p t) d -> p (t d)", p=P), g.zeros[:, :]).then_inc(g.acc_done[k], 16)
            pool.wait_ge(const_set, 4)
            nc.gpsimd.affine_select(out=g.identF[:, :], in_=g.identF[:, :], compare_op=ALU.not_equal, fill=1.0,
                                    base=0, pattern=[[-1, P]], channel_multiplier=1).then_inc(const_sel, 1)
            nc.gpsimd.affine_select(out=g.identB[:, :], in_=g.identB[:, :], compare_op=ALU.not_equal, fill=1.0,
                                    base=0, pattern=[[-1, P]], channel_multiplier=1).then_inc(const_sel, 1)
            nc.gpsimd.affine_select(out=g.sel[:, :, :], in_=g.sel[:, :, :], compare_op=ALU.not_equal, fill=128.0,
                                    base=0, pattern=[[-1, CT], [0, P]], channel_multiplier=1).then_inc(const_sel, 1)
            pool.wait_ge(const_sel, 3)
            nc.gpsimd.affine_select(out=g.sel[:, :, :], in_=g.sel[:, :, :], compare_op=ALU.not_equal, fill=1.0,
                                    base=-CT, pattern=[[-1, CT], [0, P]], channel_multiplier=1).then_inc(const_sel, 1)

        @block.vector
        def _(dve):
            steps = [0]

            def then(ins_):
                steps[0] += 1
                ins_.then_inc(v_step, 1)
                dve.wait_ge(v_step, steps[0])

            nc.vector.memset(g.xres[96:P, :], 0.0)
            dve.wait_ge(dst_in, 16)
            then(nc.vector.tensor_copy(g.dstF[:, :, :], idx_i[:, 1, :, :]))
            nc.vector.tensor_reduce(ext[:, 0, :], g.dstF[:, :, :], AX_X, ALU.min).then_inc(ext_ready, 1)
            nc.vector.tensor_reduce(ext[:, 1, :], g.dstF[:, :, :], AX_X, ALU.max).then_inc(ext_ready, 1)
            dve.wait_ge(src_in, 16)
            nc.vector.tensor_single_scalar(idx_i[:, 1, :, :], idx_i[:, 0, :, :], 7,
                                           ALU.arith_shift_right).then_inc(digit_ready, 1)
            nc.vector.tensor_single_scalar(digit[:, :, :], idx_i[:, 0, :, :], 127, ALU.bitwise_and).then_inc(digit_ready, 1)
            dve.wait_ge(ext_turned, 1)
            nc.vector.tensor_reduce(colx[0:g.NC, 0:1], ps_t[0:g.NC, 0, 0:P], AX_X, ALU.min)
            then(nc.vector.tensor_reduce(colx[0:g.NC, 1:2], ps_t[0:g.NC, 1, 0:P], AX_X, ALU.max))
            then(nc.vector.tensor_copy(colb[0:g.NC, :, :], bcast(colx[0:g.NC, :], 2, P)))
            nc.vector.tensor_copy(colb[0:g.NC, 0, 0:1], colx[0:g.NC, 0:1]).then_inc(col_ready, 1)
            dve.wait_ge(ext_spread, 1)
            nc.vector.tensor_copy(g.minB[:, :], ps_t[:, 0, 0:g.NC])
            nc.vector.tensor_copy(g.tab_min[:, :], ps_t[:, 0, 0:g.NC])
            then(nc.vector.tensor_copy(g.tab_nw[:, :], ps_t[:, 1, 0:g.NC]))
            then(nc.vector.tensor_tensor(g.tab_nw[:, :], g.tab_nw[:, :], g.tab_min[:, :], ALU.subtract))
            then(nc.vector.tensor_single_scalar(g.tab_nw[:, :], g.tab_nw[:, :], 7, ALU.arith_shift_right))
            nc.vector.tensor_single_scalar(g.tab_nw[:, :], g.tab_nw[:, :], 1, ALU.add)
            o = WIN + g.NW
            dve.wait_ge(iota_done, 5)
            nc.vector.tensor_copy(g.iota_w[:, :], int_c[:, 0:WIN])
            nc.vector.tensor_copy(g.win_off[:, :], int_c[:, WIN:o])
            nc.vector.tensor_copy(g.trash[:, :], int_c[:, o:o + 1])
            nc.vector.tensor_copy(g.pow_col[:, :], int_c[:, o + 1:o + 2].bitcast(F32))
            nc.vector.tensor_copy(g.pow_lim[:, :], int_c[:, o + 2:o + 3].bitcast(F32))
            dve.wait_ge(w_turned, 1)
            nc.vector.tensor_copy(g.V1T[:, :], ps_w[0:g.D, 0, 0:g.D])
            nc.vector.tensor_scalar_mul(g.Wc1T[:, :], ps_w[:, 1, 0:g.D], 0.5)
            for k in range(2):
                lo = slice(k * g.D, (k + 1) * g.D)
                nc.vector.memset(g.Wc2d[lo, 1 - k, :], 0.0)
                nc.vector.tensor_scalar_mul(g.Wc2d[lo, k, :], ps_w[lo, 2, 0:g.D], 2.0)
            nc.vector.tensor_scalar_mul(g.V2T[:, :], ps_w[0:g.D, 3, 0:g.D], 0.5)
            nc.vector.tensor_scalar_mul(g.V3T[:, :], ps_w[0:g.D, 4, 0:g.D], 2.0)
            nc.vector.tensor_scalar_mul(g.bc1h[:, :], g.bc1h[:, :], 0.5)
            nc.vector.tensor_scalar_mul(g.v2h[:, :], g.v2h[:, :], 0.5)
            dve.wait_ge(bias_in, 48)
            for k, ins_ in enumerate(split_steps(nc, [bias_part[:, k] for k in range(3)],
                                                 [bias_left[:, k] for k in range(2)], bias[:, :, :])):
                if k < 4:
                    then(ins_())
                else:
                    ins_().then_inc(bias_split, 1)

        @block.tensor
        def _(pe):
            pe.wait_ge(const_sel, 4)
            pe.wait_ge(ext_ready, 2)
            nc.tensor.transpose(ps_t[0:g.NC, 0, 0:P], ext[:, 0, :], g.identF[:, :])
            nc.tensor.transpose(ps_t[0:g.NC, 1, 0:P], ext[:, 1, :], g.identF[:, :]).then_inc(ext_turned, 1)
            pe.wait_ge(col_ready, 1)
            for i in range(2):
                last = nc.tensor.matmul(ps_t[:, i, 0:g.NC], colb[0:g.NC, i, :], g.identF[0:g.NC, 0:g.NC],
                                        start=True, stop=True)
            last.then_inc(ext_spread, 1)
            pe.wait_ge(w_in, 16 * 12)
            for i in range(5):
                n = P if i in (1, 2) else g.D
                last = nc.tensor.transpose(ps_w[0:n, i, 0:g.D], wload[:, i, 0:n], g.identF[0:g.D, 0:g.D])
            last.then_inc(w_turned, 1)


def each_unit(eng, g, name):
    done = eng.alloc_register(name)
    eng.reg_mov(done, 0)
    with eng.Fori(0, g.NC) as c:
        windows = eng.value_load(g.tab_nw[0:1, bass.ds(c, 1)], min_val=1, max_val=g.NW)
        with eng.Fori(0, windows) as w:
            yield c, w, eng.snap(done, min_val=0, max_val=g.NC * g.NW)
            eng.reg_add(done, done, 1)
    yield None, None, eng.snap(done, min_val=0, max_val=g.NC * g.NW)


def window_base(eng, g, c, w, name):
    first = eng.value_load(g.tab_min[0:1, bass.ds(c, 1)], min_val=0, max_val=g.N - 1)
    base = eng.alloc_register(name)
    eng.reg_mov(base, first + w * WIN)
    return eng.snap(base, min_val=0, max_val=g.N - 1)


def layer0_edges(nc, g):
    with ExitStack() as ctx:
        def sb(name, shape, dt):
            return ctx.enter_context(nc.sbuf_tensor(name, shape, dt))

        def ps(name, shape, dt):
            return ctx.enter_context(nc.psum_tensor(name, shape, dt))

        def sem(name):
            return ctx.enter_context(nc.semaphore(name))

        x_win = sb("x_win", [WIN, g.D], F32)
        x_part = sb("x_part", [WIN, 3, g.D], BF16)
        x_left = sb("x_left", [WIN, 2, g.D], F32)
        cur_hl = sb("cur_hl", [P, 2 * CT], BF16)
        cur_src = sb("cur_src", [P, CT], F32)
        cur_dst = sb("cur_dst", [P, CT], F32)
        to_trash = sb("to_trash", [P, CT], F32)
        src_rows = sb("src_rows", [2 * CT, P], BF16)
        oh = sb("oh", [P, CT, WIN], BF16)
        eq = sb("eq", [P, CT, P], BF16)
        counts = sb("counts", [WIN, GT, P], BF16)
        moved = sb("moved", [P, CT], F32)
        target = sb("target", [P, CT], I32)
        rows = sb("rows", [P, CT, g.D], F32)
        ps_hl = ps("ps_hl", [2 * CT, P], BF16)
        ps_src = ps("ps_src", [P, 2 * BANK], F32)
        ps_cnt = ps("ps_cnt", [P, 2 * BANK], F32)
        ps_first = ps("ps_first", [P, BANK], F32)
        ps_rows = ps("ps_rows", [P, BANK], F32)
        spread = ps_src[:, 0:GT * P].rearrange("p (t e) -> p t e", t=GT)
        cnt = ps_cnt[:, 0:GT * P].rearrange("p (t e) -> p t e", t=GT)
        sums = ps_rows[:, 0:GT * g.D].rearrange("p (t d) -> p t d", t=GT)

        x_win_in = sem("x_win_in")
        split_step = sem("split_step")
        x_in = sem("x_in")
        cur_ready = sem("cur_ready")
        hl_turned = sem("hl_turned")
        hl_copied = sem("hl_copied")
        spread_done = sem("spread_done")
        eq_ready = sem("eq_ready")
        cnt_done = sem("cnt_done")
        cnt_copied = sem("cnt_copied")
        sums_done = sem("sums_done")
        rows_ready = sem("rows_ready")
        mark_ready = sem("mark_ready")
        target_ready = sem("target_ready")
        rows_free = sem("rows_free")

        block = ctx.enter_context(nc.Block())

        @block.sync
        def _(sp):
            for c, w, u in each_unit(sp, g, "sp_unit"):
                if c is None:
                    continue
                base = window_base(sp, g, c, w, "sp_base")
                sp.wait_ge(split_step, u * SPLIT + SPLIT)
                sp.dma_start(x_win[:, :], g.xp[bass.ds(base, WIN), :]).then_inc(x_win_in, 16)

        @block.vector
        def _(dve):
            def one_hot(j):
                t = slice(j * GT, (j + 1) * GT)
                return nc.vector.tensor_tensor(oh[:, t, :], bcast(g.iota_w[:, :], 1, GT),
                                               bcast(cur_dst[:, t], 2, WIN), ALU.is_equal)

            dve.sem_inc(target_ready, 1)
            dve.sem_inc(split_step, SPLIT)
            split = split_steps(nc, [x_part[:, k, :] for k in range(3)], [x_left[:, k, :] for k in range(2)], x_win[:, :])
            for c, w, u in each_unit(dve, g, "dve_unit"):
                if c is None:
                    continue
                G = dve.snap(u * GR)
                dve.wait_ge(target_ready, G + 1)
                nc.vector.tensor_copy(cur_hl[:, :], g.src_hl[:, bass.ds(c, 1), :].rearrange("p a t -> p (a t)"))
                src_c = g.srcF[:, bass.ds(c, 1), :].rearrange("p a t -> p (a t)")
                dst_c = g.dstF[:, bass.ds(c, 1), :].rearrange("p a t -> p (a t)")
                nc.vector.tensor_copy(cur_src[:, :], src_c)
                nc.vector.tensor_scalar(to_trash[:, :], src_c, -1.0, g.trash[:, 0:1], ALU.mult, ALU.add)
                nc.vector.tensor_scalar(cur_dst[:, :], dst_c, g.minB[:, bass.ds(c, 1)],
                                        g.win_off[:, bass.ds(w, 1)], ALU.subtract, ALU.subtract).then_inc(cur_ready, 1)
                dve.wait_ge(cur_ready, u + 1)
                one_hot(0)
                for j in range(GR):
                    t = slice(j * GT, (j + 1) * GT)
                    dve.wait_ge(spread_done, G + (j + 1))
                    nc.vector.tensor_tensor(eq[:, t, :], spread, bcast(cur_src[:, t], 2, P),
                                            ALU.is_equal).then_inc(eq_ready, 1)
                    if j == 0:
                        dve.wait_ge(x_win_in, u * 16 + 16)
                        dve.wait_ge(sums_done, u * GR + GR)
                        for k in range(SPLIT):
                            dve.wait_ge(split_step, u * SPLIT + (SPLIT + k))
                            split[k]().then_inc(split_step, 1)
                    if j + 1 < GR:
                        one_hot(j + 1)
                    dve.wait_ge(cnt_done, G + (j + 1))
                    nc.vector.scalar_tensor_tensor(out=moved[:, t], in0=ps_first[:, t], scalar=g.pow_lim[:, 0:1],
                                                   in1=to_trash[:, t], op0=ALU.is_gt, op1=ALU.mult).then_inc(mark_ready, 1)
                    dve.wait_ge(mark_ready, G + (j + 1))
                    dve.wait_ge(rows_free, G + (j + 1))
                    nc.vector.tensor_tensor(target[:, t], moved[:, t], cur_src[:, t], ALU.add).then_inc(target_ready, 1)

        @block.scalar
        def _(act):
            act.sem_inc(rows_ready, 1)
            act.wait_ge(x_win_in, 16)
            load_nodes(act, g, g.xres, g.ins["x"], x_in)
            for c, w, u in each_unit(act, g, "act_unit"):
                if c is None:
                    continue
                G = act.snap(u * GR)
                act.wait_ge(hl_turned, u + 1)
                nc.scalar.copy(src_rows[:, :], ps_hl[:, :]).then_inc(hl_copied, 1)
                for j in range(GR):
                    t = slice(j * GT, (j + 1) * GT)
                    act.wait_ge(cnt_done, G + (j + 1))
                    nc.scalar.copy(counts[:, :, :], cnt).then_inc(cnt_copied, 1)
                    act.wait_ge(sums_done, G + (j + 1 + GR))
                    act.wait_ge(rows_free, G + (j + 1))
                    nc.scalar.copy(rows[:, t, :], sums).then_inc(rows_ready, 1)
            act.wait_ge(x_in, 48)

        @block.tensor
        def _(pe):
            def spread_group(j):
                for i in range(GT):
                    last = nc.tensor.matmul(spread[:, i, :], g.sel[:, j * GT + i, :], src_rows[:, :],
                                            start=True, stop=True)
                last.then_inc(spread_done, 1)

            pe.sem_inc(sums_done, GR)
            for c, w, u in each_unit(pe, g, "pe_unit"):
                if c is None:
                    continue
                G = pe.snap(u * GR)
                wait_alone(pe, cur_ready, u + 1, g.pe_turn)
                nc.tensor.transpose(ps_hl[:, :], cur_hl[:, :], g.identB[:, :]).then_inc(hl_turned, 1)
                pe.wait_ge(hl_copied, u + 1)
                spread_group(0)
                for j in range(GR):
                    pe.wait_ge(eq_ready, G + (j + 1))
                    for i in range(GT):
                        nc.tensor.matmul(cnt[:, i, :], oh[:, j * GT + i, :], eq[:, j * GT + i, :],
                                         start=True, stop=True)
                    for i in range(GT):
                        s = j * GT + i
                        last = nc.tensor.matmul(ps_first[:, s:s + 1], eq[:, s, :], g.pow_col[:, :],
                                                start=True, stop=True)
                    last.then_inc(cnt_done, 1)
                    if j + 1 < GR:
                        spread_group(j + 1)
                    pe.wait_ge(cnt_copied, G + (j + 1))
                    if j == 0:
                        pe.wait_ge(split_step, u * SPLIT + 2 * SPLIT)
                    pe.wait_ge(rows_ready, G + (j + 1))
                    for i in range(GT):
                        for part in range(3):
                            last = nc.tensor.matmul(sums[:, i, :], counts[:, i, :], x_part[:, part, :],
                                                    start=(part == 0), stop=(part == 2))
                    last.then_inc(sums_done, 1)

        @block.gpsimd
        def _(pool):
            pool.sem_inc(rows_free, GR - 1)
            for c, w, u in each_unit(pool, g, "pool_unit"):
                G = pool.snap(u * GR)
                if c is None:
                    for k in range(ACCS):
                        pool.wait_ge(g.acc_done[k], G * 16 + 16)
                    continue
                for j in range(GR):
                    pool.wait_ge(rows_ready, G + (j + 2))
                    pool.wait_ge(target_ready, G + (j + 2))
                    before = pool.snap(G * 16 + 16 * (j + 1))
                    for i in range(GT):
                        s = j * GT + i
                        wait_alone(pool, g.acc_done[i], before, g.pool_turn)
                        pool.indirect_dma_start(g.acc[i][:, :], bass.IndirectOffsetOnAxis(target[:, s:s + 1], 0),
                                                rows[:, s, :], None, compute_op=ALU.add).then_inc(g.acc_done[i], 16)
                    pool.sem_inc(rows_free, 1)


def layer_norm(nc, g, r, d, sq, stat, out):
    return (lambda: nc.vector.tensor_reduce(stat[:, 0, :], r, AX_X, ALU.add),
            lambda: nc.vector.tensor_scalar_mul(stat[:, 1, :], stat[:, 0, :], 1.0 / g.D),
            lambda: nc.vector.tensor_tensor(d, r, bcast(stat[:, 1, :], 2, g.D), ALU.subtract),
            lambda: nc.vector.tensor_tensor(sq, d, d, ALU.mult),
            lambda: nc.vector.tensor_reduce(stat[:, 2, :], sq, AX_X, ALU.add),
            lambda: nc.vector.tensor_scalar(stat[:, 3, :], stat[:, 2, :], 1.0 / g.D, EPS, ALU.mult, ALU.add),
            lambda: nc.vector.reciprocal(stat[:, 5, :], stat[:, 4, :]),
            lambda: nc.vector.tensor_tensor(out, d, bcast(stat[:, 5, :], 2, g.D), ALU.mult))


LN_STEPS = 8
LN_SQRT = 6


def node_phase0(nc, g):
    PAIRS = g.NB // 2
    C = BT * g.D
    H = BT * P // 2
    L = range(2)
    assert ACCS == 5
    with ExitStack() as ctx:
        def sb(name, shape, dt=F32):
            return [ctx.enter_context(nc.sbuf_tensor(f"{name}{h}", shape, dt)) for h in L]

        def sem(name):
            return [ctx.enter_context(nc.semaphore(f"{name}{h}")) for h in L]

        parts = sb("agg_in_sb", [P, ACCS, C])
        total = sb("total", [P, C])
        sT = sb("sT", [g.D, 2 * H])
        hT = sb("hT", [g.HID, 2, H])
        r = sb("r0", [P, BT, g.D])
        d = sb("d0", [P, BT, g.D])
        sq = sb("sq0", [P, BT, g.D])
        stat = sb("stat0", [P, 6, BT])
        x1 = sb("x1", [P, BT, g.D])
        x1T = sb("x1T", [g.D, 2 * H])
        nn = sb("nn", [P, C])
        ps_t = [ctx.enter_context(nc.psum_tensor(f"ps_turn{h}", [P, 2 * BANK], F32)) for h in L]
        ps_p = [ctx.enter_context(nc.psum_tensor(f"ps_prod{h}", [P, 2, BANK], F32)) for h in L]

        agg_in = sem("agg_in")
        paired = sem("paired")
        added = sem("added")
        s_turned = sem("s_turned")
        s_copied = sem("s_copied")
        h_done = sem("h_done")
        relu_done = sem("relu_done")
        y_done = sem("y_done")
        r_ready = sem("r_ready")
        ln_step = sem("ln_step0")
        std_ready = sem("std_ready0")
        x1_turned = sem("x1_turned")
        x1_copied = sem("x1_copied")
        x1_kept = sem("x1_kept")
        nn_done = sem("nn_done")
        nn_copied = sem("nn_copied")
        nn_out = sem("nn_out")
        cf_zero = ctx.enter_context(nc.semaphore("cf_zero"))

        acc_v = [a[0:P * g.NT, :].rearrange("(p t) d -> p (t d)", t=g.NT) for a in g.acc]
        nn_v = g.nn[0:P * g.NT, :].rearrange("(p t) d -> p (t d)", t=g.NT)
        block = ctx.enter_context(nc.Block())

        @block.sync
        def _(sp):
            for h in L:
                for k in range(ACCS):
                    sp.dma_start(parts[h][:, k, :], acc_v[k][:, h * C:(h + 1) * C]).then_inc(agg_in[h], 16)
            with sp.Fori(0, PAIRS - 1) as v:
                for h in L:
                    sp.wait_ge(added[h], v * 2 + 2)
                    for k in range(ACCS):
                        sp.dma_start(parts[h][:, k, :], acc_v[k][:, bass.ds((v * 2 + (h + 2)) * C, C)]).then_inc(agg_in[h], 16)
            sp.dma_start(g.cf.rearrange("(p t) d -> p (t d)", p=P), g.zeros[:, :]).then_inc(cf_zero, 16)
            sp.wait_ge(cf_zero, 16)

        @block.gpsimd
        def _(pool):
            with pool.Fori(0, PAIRS) as v:
                for k in (1, 3):
                    for h in L:
                        pool.wait_ge(agg_in[h], (v + 1) * (16 * ACCS))
                        nc.gpsimd.tensor_tensor(parts[h][:, k, :], parts[h][:, k, :], parts[h][:, k + 1, :],
                                                ALU.add).then_inc(paired[h], 1)

        @block.vector
        def _(dve):
            def x_cols(v):
                return [g.xres[:, bass.ds(held(dve, (v * 2 + h) * C), C)] for h in L]

            def add_up(v):
                for h in L:
                    dve.wait_ge(agg_in[h], (v + 1) * (16 * ACCS))
                    dve.wait_ge(paired[h], v * 2 + 1)
                    dve.wait_ge(s_turned[h], v + 1)
                    nc.vector.tensor_tensor(total[h][:, :], parts[h][:, 0, :], parts[h][:, 1, :],
                                            ALU.add).then_inc(added[h], 1)
                for h in L:
                    dve.wait_ge(paired[h], v * 2 + 2)
                    dve.wait_ge(added[h], v * 2 + 1)
                    nc.vector.tensor_tensor(total[h][:, :], total[h][:, :], parts[h][:, 3, :],
                                            ALU.add).then_inc(added[h], 1)

            def residual(v):
                x = x_cols(v)
                for h in L:
                    dve.wait_ge(y_done[h], v + 1)
                    dve.wait_ge(ln_step[h], v * LN_STEPS + 1)
                    nc.vector.tensor_tensor(r[h][:, :, :].rearrange("p t d -> p (t d)"), ps_p[h][:, 0, 0:C], x[h],
                                            ALU.add).then_inc(r_ready[h], 1)

            def normalise(v):
                steps = [layer_norm(nc, g, r[h][:, :, :], d[h][:, :, :], sq[h][:, :, :], stat[h], x1[h][:, :, :])
                         for h in L]
                for k in range(LN_STEPS):
                    for h in L:
                        if k == 0:
                            dve.wait_ge(r_ready[h], v + 2)
                        elif k == LN_SQRT:
                            dve.wait_ge(std_ready[h], v + 1)
                        else:
                            dve.wait_ge(ln_step[h], v * LN_STEPS + (k + 1))
                        if k == LN_STEPS - 1:
                            dve.wait_ge(x1_kept[h], v + 1)
                            dve.wait_ge(x1_turned[h], v + 1)
                        steps[h][k]().then_inc(ln_step[h], 1)

            for h in L:
                dve.sem_inc(ln_step[h], 1)
                dve.sem_inc(r_ready[h], 1)
            add_up(0)
            add_up(1)
            residual(0)
            with dve.Fori(0, PAIRS - 2) as v:
                normalise(v)
                add_up(v + 2)
                residual(v + 1)
            normalise(PAIRS - 2)
            residual(PAIRS - 1)
            normalise(PAIRS - 1)

        @block.scalar
        def _(act):
            def copy_s(v):
                for h in L:
                    act.wait_ge(s_turned[h], v + 2)
                    nc.scalar.copy(sT[h][:, :], ps_t[h][0:g.D, 0:2 * H]).then_inc(s_copied[h], 1)

            def root(v):
                for h in L:
                    act.wait_ge(ln_step[h], v * LN_STEPS + (LN_SQRT + 1))
                    nc.scalar.sqrt(stat[h][:, 4, :], stat[h][:, 3, :]).then_inc(std_ready[h], 1)

            def relu(v):
                for h in L:
                    act.wait_ge(h_done[h], v + 1)
                    nc.scalar.activation(hT[h][:, :, :], ps_p[h][:, :, 0:H], ACT.Relu,
                                         bias=g.b1[:, 0:1]).then_inc(relu_done[h], 1)

            def keep_and_store(v):
                col = [held(act, (v * 2 + h) * C) for h in L]
                for h in L:
                    act.wait_ge(ln_step[h], v * LN_STEPS + (LN_STEPS + 1))
                    nc.scalar.copy(g.xres[:, bass.ds(col[h], C)],
                                   x1[h][:, :, :].rearrange("p t d -> p (t d)")).then_inc(x1_kept[h], 1)
                for h in L:
                    act.wait_ge(x1_turned[h], v + 2)
                    nc.scalar.copy(x1T[h][:, :], ps_t[h][0:g.D, 0:2 * H]).then_inc(x1_copied[h], 1)
                for h in L:
                    act.wait_ge(nn_done[h], v + 1)
                    act.wait_ge(nn_out[h], (v + 1) * 16)
                    nc.scalar.copy(nn[h][:, :], ps_p[h][:, 1, 0:C]).then_inc(nn_copied[h], 1)
                for h in L:
                    act.wait_ge(nn_copied[h], v + 3)
                    act.dma_start(nn_v[:, bass.ds(col[h], C)], nn[h][:, :]).then_inc(nn_out[h], 16)

            for h in L:
                act.sem_inc(nn_out[h], 16)
                act.sem_inc(nn_copied[h], 2)
                act.sem_inc(x1_kept[h], 1)
            act.preload_act_table_set("sqrt_and_others")
            copy_s(0)
            relu(0)
            with act.Fori(0, PAIRS - 1) as v:
                copy_s(v + 1)
                root(v)
                relu(v + 1)
                keep_and_store(v)
            root(PAIRS - 1)
            keep_and_store(PAIRS - 1)
            for h in L:
                act.wait_ge(nn_out[h], 16 * (PAIRS + 1))

        @block.tensor
        def _(pe):
            def products(v):
                for h in L:
                    wait_alone(pe, added[h], v * 2 + 2, g.pe_turn)
                    for t in range(BT):
                        last = nc.tensor.transpose(ps_t[h][0:g.D, t * P:(t + 1) * P], total[h][:, t * g.D:(t + 1) * g.D],
                                                   g.identF[:, :])
                    last.then_inc(s_turned[h], 1)
                for h in L:
                    pe.wait_ge(s_copied[h], v + 1)
                    pe.wait_ge(nn_copied[h], v + 1)
                    pe.wait_ge(r_ready[h], v + 1)
                    for k in range(2):
                        last = nc.tensor.matmul(ps_p[h][:, k, 0:H], g.W1[:, :], sT[h][:, k * H:(k + 1) * H],
                                                start=True, stop=True)
                    last.then_inc(h_done[h], 1)
                for h in L:
                    y = ps_p[h][:, 0, 0:C]
                    pe.wait_ge(relu_done[h], v + 1)
                    nc.tensor.matmul(y, g.ones3[:, :], g.b2p[:, :, :].rearrange("o t d -> o (t d)"),
                                     start=True, stop=False, skip_group_check=True)
                    hv = hT[h][:, :, :].rearrange("p a b -> p (a b)")
                    for t in range(BT):
                        last = nc.tensor.matmul(y[:, t * g.D:(t + 1) * g.D], hv[:, t * P:(t + 1) * P], g.W2[:, :],
                                                start=False, stop=(t == BT - 1), skip_group_check=True)
                    last.then_inc(y_done[h], 1)

            def new_node(v):
                for h in L:
                    wait_alone(pe, ln_step[h], v * LN_STEPS + (LN_STEPS + 1), g.pe_turn)
                    for t in range(BT):
                        last = nc.tensor.transpose(ps_t[h][0:g.D, t * P:(t + 1) * P], x1[h][:, t, :], g.identF[:, :])
                    last.then_inc(x1_turned[h], 1)
                for h in L:
                    pe.wait_ge(x1_copied[h], v + 1)
                    for t in range(BT):
                        last = nc.tensor.matmul(ps_p[h][:, 1, t * g.D:(t + 1) * g.D], x1T[h][:, t * P:(t + 1) * P],
                                                g.V1T[:, :], start=True, stop=True)
                    last.then_inc(nn_done[h], 1)

            for h in L:
                pe.sem_inc(s_turned[h], 1)
                pe.sem_inc(x1_turned[h], 1)
            products(0)
            with pe.Fori(0, PAIRS - 1) as v:
                products(v + 1)
                new_node(v)
            new_node(PAIRS - 1)


def layer1_edges(nc, g):
    HALF = GT * P // 2
    MID = GT // 2
    ZB = 3
    with ExitStack() as ctx:
        def sb(name, shape, dt=F32):
            return ctx.enter_context(nc.sbuf_tensor(name, shape, dt))

        def ps(name, shape):
            return ctx.enter_context(nc.psum_tensor(name, shape, F32))

        def sem(name):
            return ctx.enter_context(nc.semaphore(name))

        ea = sb("ea", [P, CT, g.F])
        ea_T = sb("ea_T", [g.F, 2, HALF])
        cur_dst = sb("cur_dst1", [P, CT])
        oh = sb("oh1", [P, CT, WIN])
        y_cap = sb("y_cap", [P, HALF])
        e_y = sb("e_y", [P, HALF])
        q = sb("q", [P, HALF])
        sp_y = sb("sp_y", [P, GR, HALF])
        idx = sb("idx", [P, CT], I32)
        nn = sb("nn_rows", [P, CT, g.D])
        msg = sb("msg", [P, CT, g.D])
        seg = sb("seg", [WIN, g.D])
        cf_old = sb("cf_old", [WIN, g.D])
        ps_t = ps("ps_t", [P, 2, BANK])
        ps_z = ps("ps_z", [P, ZB, BANK])
        ps_e = ps("ps_e", [P, 2, BANK])
        ps_seg = ps("ps_seg", [P, BANK])

        ea_in = [sem(f"ea_in{j}") for j in range(GR)]
        idx_in = [sem(f"idx_in{j}") for j in range(GR)]
        gathered = [sem(f"gathered{j}") for j in range(GR)]
        turned = sem("turned")
        turn_copied = sem("turn_copied")
        z_done = sem("z_done")
        capped = sem("capped")
        exp_done = sem("exp_done")
        log_done = sem("log_done")
        sp_ready = sem("sp_ready")
        h_done = sem("h_done1")
        msg_ready = sem("msg_ready")
        dst_ready = sem("dst_ready")
        seg_group = sem("seg_group")
        seg_ready = sem("seg_ready")
        cf_in = sem("cf_old_in")
        cf_out = sem("cf_out")

        src_v = g.ins["src"].rearrange("(c p t) -> p c t", p=P, t=CT)
        ea_v = g.ins["edge_attr_128"].rearrange("(c p t) f -> c p (t f)", p=P, t=CT)
        block = ctx.enter_context(nc.Block())

        @block.sync
        def _(sp):
            def load_attributes(c, j, G):
                sp.wait_ge(turned, G + (j + 1))
                sp.dma_start(ea[:, j * GT:(j + 1) * GT, :].rearrange("p t f -> p (t f)"),
                             ea_v[bass.ds(c, 1), :, j * GT * g.F:(j + 1) * GT * g.F].rearrange("a p f -> (a p) f")
                             ).then_inc(ea_in[j], 16)

            last_base = sp.alloc_register("last_base")
            sp.reg_mov(last_base, 0)

            def store_window(u):
                sp.wait_ge(seg_ready, u + 1)
                last = sp.snap(last_base, min_val=0, max_val=g.N - 1)
                sp.dma_start(g.cf[bass.ds(last, WIN), :], seg[:, :]).then_inc(cf_out, 16)
                wait_alone(sp, cf_out, u * 16 + 16, g.sp_turn)

            for c, w, u in each_unit(sp, g, "sp_unit1"):
                G = sp.snap(u * GR)
                if c is None:
                    for j in range(2):
                        load_attributes(0, j, G)
                    store_window(u)
                    continue
                base = window_base(sp, g, c, w, "sp_base1")
                for j in range(GR):
                    load_attributes(c, j, G)
                    sp.wait_ge(msg_ready, G + (j + 1))
                    with nc.allow_non_contiguous_dma("five indices a partition"):
                        sp.dma_start(idx[:, j * GT:(j + 1) * GT],
                                     src_v[:, bass.ds(c, 1), j * GT:(j + 1) * GT].rearrange("p a t -> p (a t)")
                                     ).then_inc(idx_in[j], 16)
                store_window(u)
                sp.dma_start(cf_old[:, :], g.cf[bass.ds(base, WIN), :]).then_inc(cf_in, 16)
                sp.reg_mov(last_base, base)

        @block.gpsimd
        def _(pool):
            for c, w, u in each_unit(pool, g, "pool_unit1"):
                if c is None:
                    continue
                G = pool.snap(u * GR)
                for j in range(GR):
                    pool.wait_ge(idx_in[j], u * 16 + 16)
                    wait_alone(pool, msg_ready, G + (j + 1), g.pool_turn)
                    for i in range(GT):
                        s = j * GT + i
                        pool.indirect_dma_start(nn[:, s, :], None, g.nn[0:g.N, :],
                                                bass.IndirectOffsetOnAxis(idx[:, s:s + 1], 0)).then_inc(gathered[j], 16)

        @block.vector
        def _(dve):
            def message(j, G, u):
                t = slice(j * GT, (j + 1) * GT)
                dve.wait_ge(h_done, G + (j + 1))
                dve.wait_ge(gathered[j], u * (16 * GT) + 16 * GT)
                nc.vector.tensor_tensor(msg[:, t, :], ps_e[:, j % 2, 0:GT * g.D].rearrange("p (t d) -> p t d", d=g.D),
                                        nn[:, t, :], ALU.mult).then_inc(msg_ready, 1)

            def cap(j, G):
                dve.wait_ge(z_done, G + (j + 1))
                nc.vector.tensor_scalar(y_cap[:, :], ps_z[:, j % GR % ZB, 0:HALF], g.bc1h[:, 0:1], CAP,
                                        ALU.add, ALU.min).then_inc(capped, 1)

            def softplus(j, G):
                dve.wait_ge(log_done, G + (j + 1))
                nc.vector.scalar_tensor_tensor(out=sp_y[:, j % GR, :], in0=ps_z[:, j % GR % ZB, 0:HALF],
                                               scalar=g.bc1h[:, 0:1], in1=q[:, :],
                                               op0=ALU.add, op1=ALU.max).then_inc(sp_ready, 1)

            dve.sem_inc(msg_ready, GR)
            nc.vector.memset(seg[:, :], 0.0).then_inc(seg_ready, 1)
            cap(0, 0)
            softplus(0, 0)
            for c, w, u in each_unit(dve, g, "dve_unit1"):
                if c is None:
                    continue
                G = dve.snap(u * GR)
                dst_c = g.dstF[:, bass.ds(c, 1), :].rearrange("p a t -> p (a t)")
                dve.wait_ge(msg_ready, G + GR)
                nc.vector.tensor_scalar(cur_dst[:, :], dst_c, g.minB[:, bass.ds(c, 1)],
                                        g.win_off[:, bass.ds(w, 1)], ALU.subtract, ALU.subtract).then_inc(dst_ready, 1)
                for j in range(GR):
                    t = slice(j * GT, (j + 1) * GT)
                    cap(j + 1, G)
                    if j == 0:
                        dve.wait_ge(dst_ready, u + 1)
                    dve.wait_ge(seg_group, G + (j + 1))
                    nc.vector.tensor_tensor(oh[:, t, :], bcast(g.iota_w[:, :], 1, GT),
                                            bcast(cur_dst[:, t], 2, WIN), ALU.is_equal)
                    if j > 0:
                        message(j - 1, G, u)
                    softplus(j + 1, G)
                message(GR - 1, G, u)
                dve.wait_ge(seg_group, G + 2 * GR)
                dve.wait_ge(cf_in, u * 16 + 16)
                nc.vector.tensor_tensor(seg[:, :], ps_seg[:, 0:g.D], cf_old[:, :], ALU.add).then_inc(seg_ready, 1)

        @block.scalar
        def _(act):
            def copy_turned(j, G):
                act.wait_ge(turned, G + (j + 1 + GR))
                nc.scalar.copy(ea_T[:, :, :], ps_t[:, :, 0:HALF]).then_inc(turn_copied, 1)

            def logarithm(j, G):
                act.wait_ge(capped, G + (j + 1))
                nc.scalar.activation(e_y[:, :], y_cap[:, :], ACT.Exp).then_inc(exp_done, 1)
                act.wait_ge(exp_done, G + (j + 1))
                nc.scalar.activation(q[:, :], e_y[:, :], ACT.Ln, bias=1.0).then_inc(log_done, 1)

            act.preload_act_table_set("natural_log_exp_and_others")
            copy_turned(0, 0)
            logarithm(0, 0)
            copy_turned(1, 0)
            for c, w, u in each_unit(act, g, "act_unit1"):
                if c is None:
                    continue
                G = act.snap(u * GR)
                for j in range(GR):
                    logarithm(j + 1, G)
                    copy_turned(j + 2, G)

        @block.tensor
        def _(pe):
            def turn(j, G, rounds):
                pe.wait_ge(ea_in[j % GR], rounds)
                for bank, at, i in ((1, HALF - P, MID), (0, 0, 0), (0, P, 1), (0, 2 * P, MID), (1, 0, 3), (1, P, 4)):
                    last = nc.tensor.transpose(ps_t[:, bank, at:at + P], ea[:, j % GR * GT + i, :], g.identF[:, :])
                last.then_inc(turned, 1)

            def first(j, G):
                pe.wait_ge(turn_copied, G + (j + 1))
                z = ps_z[:, j % GR % ZB, 0:HALF]
                nc.tensor.matmul(z[0:g.D, :], g.Wc1T[:, :], ea_T[:, 0, :], start=True, stop=True)
                nc.tensor.matmul(z[g.D:P, :], g.Wc1T[:, :], ea_T[:, 1, :], start=True, stop=True).then_inc(z_done, 1)

            def second(j, G):
                pe.wait_ge(sp_ready, G + (j + 1))
                out = ps_e[:, j % 2, 0:GT * g.D]
                nc.tensor.matmul(out, g.ones3[:, :], g.bc2p[:, :, :].rearrange("o t d -> o (t d)"),
                                 start=True, stop=False, skip_group_check=True)
                tiles = out.rearrange("p (t d) -> p t d", d=g.D)
                for i in range(MID):
                    nc.tensor.matmul(tiles[:, i:GT:MID + 1, :], sp_y[:, j, i * P:(i + 1) * P], g.Wc2d[:, :, :],
                                     start=False, stop=False, skip_group_check=True)
                for k in range(2):
                    last = nc.tensor.matmul(tiles[k * g.D:(k + 1) * g.D, MID, :], sp_y[:, j, MID * P:HALF],
                                            g.Wc2d[:, k, :], start=False, stop=True, skip_group_check=True)
                last.then_inc(h_done, 1)

            def sum_up(j, G, u):
                pe.wait_ge(msg_ready, G + (j + 1 + GR))
                if j == 0:
                    pe.wait_ge(seg_ready, u + 1)
                for i in range(GT):
                    s = j * GT + i
                    last = nc.tensor.matmul(ps_seg[:, 0:g.D], oh[:, s, :], msg[:, s, :],
                                            start=(s == 0), stop=(s == CT - 1))
                last.then_inc(seg_group, 1)

            pe.sem_inc(turned, GR)
            pe.sem_inc(seg_group, GR)
            turn(0, 0, 16)
            first(0, 0)
            turn(1, 0, 16)
            for c, w, u in each_unit(pe, g, "pe_unit1"):
                if c is None:
                    continue
                G = pe.snap(u * GR)
                for j in range(GR):
                    first(j + 1, G)
                    if j + 2 < GR:
                        turn(j + 2, G, u * 16 + 16)
                    else:
                        turn(j + 2, G, u * 16 + 32)
                    if j > 0:
                        sum_up(j - 1, G, u)
                    second(j, G)
                sum_up(GR - 1, G, u)


def node_phase1(nc, g):
    PAIRS = g.NB // 2
    C = BT * g.D
    H = BT * P // 2
    L = range(2)
    with ExitStack() as ctx:
        def sb(name, shape, dt=F32):
            return [ctx.enter_context(nc.sbuf_tensor(f"{name}{h}", shape, dt)) for h in L]

        def sem(name):
            return [ctx.enter_context(nc.semaphore(f"{name}{h}")) for h in L]

        cf = sb("cf_in_sb", [P, C])
        cT = sb("cT", [g.D, 2 * H])
        y_cap = sb("y_cap1", [g.D, 2, H])
        e_y = sb("e_y1", [g.D, 2, H])
        q = sb("q1", [g.D, 2, H])
        sp_y = sb("sp_y1", [g.D, 2, H])
        r = sb("r1", [P, BT, g.D])
        d = sb("d1", [P, BT, g.D])
        sq = sb("sq1", [P, BT, g.D])
        stat = sb("stat1", [P, 6, BT])
        ps_c = [ctx.enter_context(nc.psum_tensor(f"ps_c{h}", [g.D, 2 * BANK], F32)) for h in L]
        ps_z = [ctx.enter_context(nc.psum_tensor(f"ps_z1_{h}", [P, 2, BANK], F32)) for h in L]

        cf_in = sem("cf_in")
        c_turned = sem("c_turned")
        c_copied = sem("c_copied")
        z_done = sem("z_done2")
        capped = sem("capped2")
        exp_done = sem("exp_done2")
        log_done = sem("log_done2")
        sp_ready = sem("sp_ready2")
        y_done = sem("y_done2")
        r_ready = sem("r_ready2")
        ln_step = sem("ln_step1")
        std_ready = sem("std_ready1")
        stored = ctx.enter_context(nc.semaphore("stored"))

        cf_v = g.cf[0:P * g.NT, :].rearrange("(p t) d -> p (t d)", t=g.NT)
        P16 = (P - 1) // 16 * 16
        out_v = g.out[0:(P - 1) * g.NT, :].rearrange("(p t) d -> p (t d)", t=g.NT)
        block = ctx.enter_context(nc.Block())

        @block.sync
        def _(sp):
            def load(v):
                for h in L:
                    sp.dma_start(cf[h][:, :], cf_v[:, bass.ds((v * 2 + h) * C, C)]).then_inc(cf_in[h], 16)

            def store(v):
                for h in L:
                    sp.wait_ge(ln_step[h], v * LN_STEPS + (LN_STEPS + 1))
                cols = bass.ds(held(sp, v * (2 * C)), 2 * C)
                sp.dma_start(out_v[0:P16, cols], g.xres[0:P16, cols]).then_inc(stored, 16)
                sp.dma_start(out_v[P16:P - 1, cols], g.xres[P16:P - 1, cols]).then_inc(stored, 16)

            load(0)
            for h in L:
                sp.wait_ge(c_turned[h], 1)
            load(1)
            with sp.Fori(0, PAIRS - 2) as v:
                for h in L:
                    sp.wait_ge(c_turned[h], v + 2)
                load(v + 2)
                store(v)
            store(PAIRS - 2)
            store(PAIRS - 1)
            left = g.N - (P - 1) * g.NT
            sp.dma_start(g.out[(P - 1) * g.NT:g.N, :].rearrange("t d -> (t d)").unsqueeze(0),
                         g.xres[P - 1:P, 0:left * g.D]).then_inc(stored, 16)
            sp.wait_ge(stored, 16 * (2 * PAIRS + 1))

        @block.tensor
        def _(pe):
            def turn(v):
                for h in L:
                    wait_alone(pe, cf_in[h], (v + 1) * 16, g.pe_turn)
                    for t in range(BT):
                        last = nc.tensor.transpose(ps_c[h][:, t * P:(t + 1) * P], cf[h][:, t * g.D:(t + 1) * g.D],
                                                   g.identF[:, :])
                    last.then_inc(c_turned[h], 1)

            def first_product(v):
                for h in L:
                    pe.wait_ge(r_ready[h], v + 1)
                    wait_alone(pe, c_copied[h], v + 1, g.pe_turn)
                    for k in range(2):
                        last = nc.tensor.matmul(ps_z[h][0:g.D, k, 0:H], g.V2T[:, :], cT[h][:, k * H:(k + 1) * H],
                                                start=True, stop=True)
                    last.then_inc(z_done[h], 1)

            def second_product(v):
                for h in L:
                    y = ps_z[h][:, 0, 0:C]
                    pe.wait_ge(sp_ready[h], v + 1)
                    nc.tensor.matmul(y, g.ones3[:, :], g.v3p[:, :, :].rearrange("o t d -> o (t d)"),
                                     start=True, stop=False, skip_group_check=True)
                    sv = sp_y[h][:, :, :].rearrange("p a b -> p (a b)")
                    for t in range(BT):
                        last = nc.tensor.matmul(y[:, t * g.D:(t + 1) * g.D], sv[:, t * P:(t + 1) * P], g.V3T[:, :],
                                                start=False, stop=(t == BT - 1), skip_group_check=True)
                    last.then_inc(y_done[h], 1)

            turn(0)
            with pe.Fori(0, PAIRS - 1) as v:
                first_product(v)
                turn(v + 1)
                second_product(v)
            first_product(PAIRS - 1)
            second_product(PAIRS - 1)

        @block.scalar
        def _(act):
            def copy_c(v):
                for h in L:
                    act.wait_ge(c_turned[h], v + 1)
                    nc.scalar.copy(cT[h][:, :], ps_c[h][0:g.D, 0:2 * H]).then_inc(c_copied[h], 1)

            def root(v):
                act.preload_act_table_set("sqrt_and_others")
                for h in L:
                    act.wait_ge(ln_step[h], v * LN_STEPS + (LN_SQRT + 1))
                    nc.scalar.sqrt(stat[h][:, 4, :], stat[h][:, 3, :]).then_inc(std_ready[h], 1)

            def exp_log(v):
                act.preload_act_table_set("natural_log_exp_and_others")
                for h in L:
                    act.wait_ge(capped[h], v + 1)
                    nc.scalar.activation(e_y[h][:, :, :], y_cap[h][:, :, :], ACT.Exp).then_inc(exp_done[h], 1)
                for h in L:
                    act.wait_ge(exp_done[h], v + 1)
                    nc.scalar.activation(q[h][:, :, :], e_y[h][:, :, :], ACT.Ln, bias=1.0).then_inc(log_done[h], 1)

            copy_c(0)
            exp_log(0)
            copy_c(1)
            with act.Fori(0, PAIRS - 2) as v:
                exp_log(v + 1)
                root(v)
                copy_c(v + 2)
            exp_log(PAIRS - 1)
            root(PAIRS - 2)
            root(PAIRS - 1)

        @block.vector
        def _(dve):
            def x_cols(v):
                return [g.xres[:, bass.ds(held(dve, (v * 2 + h) * C), C)] for h in L]

            def cap(v):
                for h in L:
                    dve.wait_ge(z_done[h], v + 1)
                    nc.vector.tensor_scalar(y_cap[h][:, :, :], ps_z[h][0:g.D, :, 0:H], g.v2h[:, 0:1], CAP,
                                            ALU.add, ALU.min).then_inc(capped[h], 1)

            def softplus(v):
                for h in L:
                    dve.wait_ge(log_done[h], v + 1)
                    nc.vector.scalar_tensor_tensor(out=sp_y[h][:, :, :], in0=ps_z[h][0:g.D, :, 0:H], scalar=g.v2h[:, 0:1],
                                                   in1=q[h][:, :, :], op0=ALU.add, op1=ALU.max).then_inc(sp_ready[h], 1)

            def residual(v):
                x = x_cols(v)
                for h in L:
                    dve.wait_ge(y_done[h], v + 1)
                    dve.wait_ge(ln_step[h], v * LN_STEPS + 1)
                    nc.vector.scalar_tensor_tensor(out=r[h][:, :, :].rearrange("p t d -> p (t d)"), in0=x[h], scalar=2.0,
                                                   in1=ps_z[h][:, 0, 0:C], op0=ALU.mult, op1=ALU.add).then_inc(r_ready[h], 1)

            def normalise(v, first, end):
                x = x_cols(v)
                steps = [layer_norm(nc, g, r[h][:, :, :], d[h][:, :, :], sq[h][:, :, :], stat[h],
                                    x[h].rearrange("p (t d) -> p t d", d=g.D)) for h in L]
                for k in range(first, end):
                    for h in L:
                        if k == 0:
                            dve.wait_ge(r_ready[h], v + 2)
                        elif k == LN_SQRT:
                            dve.wait_ge(std_ready[h], v + 1)
                        else:
                            dve.wait_ge(ln_step[h], v * LN_STEPS + (k + 1))
                        steps[h][k]().then_inc(ln_step[h], 1)

            for h in L:
                dve.sem_inc(ln_step[h], 1)
                dve.sem_inc(r_ready[h], 1)
            cap(0)
            softplus(0)
            residual(0)
            with dve.Fori(0, PAIRS - 1) as v:
                normalise(v, 0, 3)
                cap(v + 1)
                normalise(v, 3, LN_SQRT)
                softplus(v + 1)
                normalise(v, LN_SQRT, LN_STEPS)
                residual(v + 1)
            normalise(PAIRS - 1, 0, LN_STEPS)


def build(nc, ins, out):
    with ExitStack() as ctx:
        g = make_plan(nc, ctx, ins, out)
        prep_phase(nc, g)
        layer0_edges(nc, g)
        node_phase0(nc, g)
        layer1_edges(nc, g)
        node_phase1(nc, g)


_INS = ["x", "src", "dst", "edge_attr_128", "L0_gnn_W1", "L0_gnn_b1", "L0_gnn_W2", "L0_gnn_b2", "L1_gnn_W1",
        "L1_gnn_Wc1", "L1_gnn_bc1", "L1_gnn_Wc2", "L1_gnn_bc2", "L1_gnn_W2", "L1_gnn_b2", "L1_gnn_W3", "L1_gnn_b3"]


def kernel(**inputs):
    import numpy as _np
    import concourse.bacc as _bacc
    from concourse import mybir as _mybir
    from concourse.bass_utils import run_bass_kernel_spmd as _run

    nc = _bacc.Bacc("TRN2", target_bir_lowering=False, num_devices=1)
    arrays, aps = {}, {}
    for name in _INS:
        a = _np.ascontiguousarray(inputs[name])
        arrays[f"in_{name}_dram"] = a
        aps[name] = nc.dram_tensor(f"in_{name}_dram", a.shape, _mybir.dt.from_np(a.dtype), kind="ExternalInput").ap()
    out = nc.dram_tensor("out_0_dram", inputs["x"].shape, _mybir.dt.float32, kind="ExternalOutput").ap()
    build(nc, aps, out)
    r = _run(nc, [arrays], core_ids=[0])
    return r.results[0]["out_0_dram"]
```

```python
from contextlib import ExitStack

import concourse.bass as bass
from concourse import mybir

F32 = mybir.dt.float32
BF16 = mybir.dt.bfloat16
I32 = mybir.dt.int32
ALU = mybir.AluOpType
ACT = mybir.ActivationFunctionType
AX_X = mybir.AxisListType.X

P = 128
GT = 5
GR = 5
CT = GT * GR
WIN = 128
ACCS = 5
BT = 7
LANE_TILES = (BT + 1, BT - 1)
LANE_AT = (0, BT + 1)
EPS = 1e-5
CAP = 20.0
BANK = 512


def bcast(ap, axis, n):
    shape = list(ap.shape)
    return ap.unsqueeze(axis).broadcast_to(shape[:axis] + [n] + shape[axis:])


def wait_alone(eng, sem, value, turn):
    eng.wait_ge(sem, value)
    eng.sem_inc(turn, 1)


def held(eng, value):
    return value if isinstance(value, int) else eng.snap(value)


def split_steps(nc, part, left, value):
    return (lambda: nc.vector.tensor_copy(part[0], value),
            lambda: nc.vector.tensor_tensor(left[0], value, part[0], ALU.subtract),
            lambda: nc.vector.tensor_copy(part[1], left[0]),
            lambda: nc.vector.tensor_tensor(left[1], left[0], part[1], ALU.subtract),
            lambda: nc.vector.tensor_copy(part[2], left[1]))


SPLIT = 5


class Plan:
    pass


def make_plan(nc, ctx, ins, out):
    g = Plan()
    g.ins, g.out = ins, out
    g.N, g.D = ins["x"].shape
    g.E, g.F = ins["edge_attr_128"].shape
    g.HID = ins["L0_gnn_W1"].shape[1]
    g.NC = g.E // (P * CT)
    g.NT = -(-g.N // P)
    g.NB = g.NT // BT
    g.NW = -(-g.N // WIN)
    g.ROWS = P * (g.NT + 1)
    assert g.E == g.NC * P * CT and g.NT == g.NB * BT and g.NB % 2 == 0
    assert g.ROWS >= g.N + P and g.ROWS >= g.N + WIN and g.D == 64 and g.F == P and g.HID == P
    assert g.NC <= P

    def dram(name, cols, dt):
        return nc.dram_tensor(name, (g.ROWS, cols), dt, kind="Internal").ap()

    g.acc = [dram(f"agg_part{k}", g.D, F32) for k in range(ACCS)]
    g.cf = dram("cf_node", g.D, F32)
    g.nn = dram("new_node", g.D, F32)
    g.xp = dram("x_padded", g.D, F32)

    def sb(name, shape, dt):
        return ctx.enter_context(nc.sbuf_tensor(name, shape, dt))

    g.identF = sb("identF", [P, P], F32)
    g.identB = sb("identB", [P, P], BF16)
    g.iota_w = sb("iota_w", [P, WIN], F32)
    g.win_off = sb("win_off", [P, g.NW], F32)
    g.pow_col = sb("pow_col", [P, 1], BF16)
    g.pow_lim = sb("pow_lim", [P, 1], F32)
    g.trash = sb("trash", [P, 1], F32)
    g.sel = sb("sel", [2 * CT, CT, P], BF16)
    g.srcF = sb("srcF", [P, g.NC, CT], F32)
    g.dstF = sb("dstF", [P, g.NC, CT], F32)
    g.src_hl = sb("src_hl", [P, g.NC, 2 * CT], BF16)
    g.minB = sb("minB", [P, g.NC], F32)
    g.tab_min = sb("tab_min", [P, g.NC], I32)
    g.tab_nw = sb("tab_nw", [P, g.NC], I32)
    g.zeros = sb("zeros", [P, g.ROWS // P * g.D], F32)
    g.xres = sb("xres", [P, g.NT * g.D], F32)
    g.W1 = sb("W1", [P, g.HID], F32)
    g.b1 = sb("b1", [g.HID, 1], F32)
    g.W2 = sb("W2", [g.HID, g.D], F32)
    g.b2p = sb("b2p", [3, LANE_TILES[0], g.D], BF16)
    g.V1d = sb("V1d", [P, 2, g.D], F32)
    g.Wc1T = sb("Wc1T", [g.F, g.D], F32)
    g.bc1h = sb("bc1h", [P, 1], F32)
    g.Wc2d = sb("Wc2d", [P, 2, g.D], F32)
    g.bc2p = sb("bc2p", [3, GT, g.D], BF16)
    g.ones3 = sb("ones3", [3, P], BF16)
    g.V2d = sb("V2d", [P, 2, g.D], F32)
    g.v2h = sb("v2h", [P, 1], F32)
    g.V3d = sb("V3d", [P, 2, g.D], F32)
    g.v3p = sb("v3p", [3, LANE_TILES[0], g.D], BF16)
    g.acc_done = [ctx.enter_context(nc.semaphore(f"acc_done{k}")) for k in range(ACCS)]
    g.pool_turn = ctx.enter_context(nc.semaphore("pool_turn"))
    g.sp_turn = ctx.enter_context(nc.semaphore("sp_turn"))
    g.pe_turn = ctx.enter_context(nc.semaphore("pe_turn"))
    return g


def load_nodes(eng, g, tile, dram, sem):
    row = g.NT * g.D
    full = g.N // g.NT
    even = full // 16 * 16
    rest = (g.N - full * g.NT) * g.D
    whole = dram[0:full * g.NT, :].rearrange("(p t) d -> p (t d)", t=g.NT)
    last = dram[full * g.NT:g.N, :].rearrange("(o t) d -> o (t d)", o=1)
    for s, d in ((tile[0:even, :], whole[0:even, :]), (tile[even:full, :], whole[even:full, :]),
                 (tile[full:full + 1, 0:rest], last)):
        eng.dma_start(s, d).then_inc(sem, 16)
    assert full + 1 == P and row == tile.shape[1]


def prep_phase(nc, g):
    ins = g.ins
    with ExitStack() as ctx:
        def sb(name, shape, dt):
            return ctx.enter_context(nc.sbuf_tensor(name, shape, dt))

        def sem(name):
            return ctx.enter_context(nc.semaphore(name))

        idx_i = sb("idx_i", [P, 2, g.NC, CT], I32)
        digit = sb("digit", [P, g.NC, CT], I32)
        int_c = sb("int_c", [P, WIN + g.NW + 3], I32)
        wload = sb("wload", [g.D, 5, P], F32)
        ext = sb("ext", [P, 2, g.NC], F32)
        colx = sb("colx", [P, 2], F32)
        colb = sb("colb", [P, 2, P], F32)
        bias = sb("bias", [1, 3, g.D], F32)
        bias_part = sb("bias_part", [1, 3, 3, g.D], BF16)
        bias_left = sb("bias_left", [1, 2, 3, g.D], F32)
        ps_t = ctx.enter_context(nc.psum_tensor("prep_t", [P, 2, BANK], F32))
        ps_w = ctx.enter_context(nc.psum_tensor("prep_w", [P, 5, P], F32))

        src_in = sem("src_in")
        dst_in = sem("dst_in")
        w_in = sem("w_in")
        zeroed = sem("zeroed")
        const_set = sem("const_set")
        const_sel = sem("const_sel")
        iota_done = sem("iota_done")
        v_step = sem("v_step")
        ext_ready = sem("ext_ready")
        ext_turned = sem("ext_turned")
        col_ready = sem("col_ready")
        ext_spread = sem("ext_spread")
        w_turned = sem("w_turned")
        xp_out = sem("xp_out")
        digit_ready = sem("digit_ready")
        bias_split = sem("bias_split")
        bias_in = sem("bias_in")
        bias_spread = sem("bias_spread")

        src_v = ins["src"].rearrange("(c p t) -> p c t", p=P, t=CT)
        dst_v = ins["dst"].rearrange("(c p t) -> p c t", p=P, t=CT)

        def flat(nodes):
            return nodes.rearrange("n d -> (n d)").rearrange("(a b) -> a b", a=10 * 16)

        block = ctx.enter_context(nc.Block())

        @block.sync
        def _(sp):
            sp.dma_start(idx_i[:, 1, :, :], dst_v).then_inc(dst_in, 16)
            sp.dma_start(idx_i[:, 0, :, :], src_v).then_inc(src_in, 16)
            sp.dma_start(flat(g.xp[0:g.N, :]), flat(ins["x"])).then_inc(xp_out, 16)
            sp.wait_ge(zeroed, 1)
            sp.dma_start(g.xp[g.N:g.N + P, :], g.zeros[:, 0:g.D]).then_inc(xp_out, 16)
            sp.dma_start(g.xp[g.N + P:g.ROWS, :], g.zeros[0:g.ROWS - g.N - P, 0:g.D]).then_inc(xp_out, 16)
            sp.dma_start(g.acc[0][g.N:g.N + P, :], g.zeros[:, 0:g.D]).then_inc(xp_out, 16)
            sp.dma_start(g.acc[0][g.N + P:g.ROWS, :], g.zeros[0:g.ROWS - g.N - P, 0:g.D]).then_inc(xp_out, 16)
            sp.wait_ge(xp_out, 80)

        @block.scalar
        def _(act):
            def small(out, in_):
                act.dma_start(out, in_).then_inc(w_in, 16)

            def column(v):
                return v.rearrange("(n o) -> n o", o=1)

            def row(v):
                return v.rearrange("(o n) -> o n", o=1)

            for k, name in enumerate(("L0_gnn_b2", "L1_gnn_bc2", "L1_gnn_b3")):
                act.dma_start(bias[:, k, :], row(ins[name])).then_inc(bias_in, 16)
            for k in range(2):
                small(g.W1[k * g.D:(k + 1) * g.D, :], ins["L0_gnn_W1"])
                small(wload[:, 0, k * g.D:(k + 1) * g.D], ins["L1_gnn_W1"])
            small(g.W2[:, :], ins["L0_gnn_W2"])
            small(g.b1[:, :], column(ins["L0_gnn_b1"]))
            small(wload[:, 1, :], ins["L1_gnn_Wc1"])
            small(wload[:, 2, 0:g.D], ins["L1_gnn_Wc2"])
            small(wload[:, 2, g.D:P], ins["L1_gnn_Wc2"])
            for k in range(2):
                small(wload[:, 3, k * g.D:(k + 1) * g.D], ins["L1_gnn_W2"])
                small(wload[:, 4, k * g.D:(k + 1) * g.D], ins["L1_gnn_W3"])
            small(g.bc1h[0:g.D, :], column(ins["L1_gnn_bc1"]))
            small(g.bc1h[g.D:P, :], column(ins["L1_gnn_bc1"]))
            small(g.v2h[0:g.D, :], column(ins["L1_gnn_b2"]))
            small(g.v2h[g.D:P, :], column(ins["L1_gnn_b2"]))
            act.wait_ge(src_in, 16)
            nc.scalar.copy(g.srcF[:, :, :], idx_i[:, 0, :, :])
            act.wait_ge(digit_ready, 1)
            nc.scalar.copy(g.src_hl[:, :, 0:CT], idx_i[:, 1, :, :])
            act.wait_ge(digit_ready, 2)
            nc.scalar.copy(g.src_hl[:, :, CT:2 * CT], digit[:, :, :])
            act.wait_ge(bias_split, 1)
            for k, (to, n) in enumerate(((g.b2p, LANE_TILES[0]), (g.bc2p, GT), (g.v3p, LANE_TILES[0]))):
                for part in range(3):
                    act.dma_start(to[part:part + 1, :, :], bcast(bias_part[:, part, k, :], 1, n)).then_inc(bias_spread, 16)
            act.wait_ge(bias_spread, 16 * 9)

        @block.gpsimd
        def _(pool):
            nc.gpsimd.memset(g.zeros[:, :], 0.0).then_inc(zeroed, 1)
            nc.gpsimd.memset(g.identF[:, :], 0.0).then_inc(const_set, 1)
            nc.gpsimd.memset(g.identB[:, :], 0.0).then_inc(const_set, 1)
            nc.gpsimd.memset(g.sel[:, :, :], 0.0).then_inc(const_set, 1)
            nc.gpsimd.memset(g.ones3[:, :], 1.0).then_inc(const_set, 1)
            o = WIN + g.NW
            nc.gpsimd.iota(int_c[:, 0:WIN], [[1, WIN]], 0, 0).then_inc(iota_done, 1)
            nc.gpsimd.iota(int_c[:, WIN:o], [[WIN, g.NW]], 0, 0).then_inc(iota_done, 1)
            nc.gpsimd.iota(int_c[:, o:o + 1], [[0, 1]], g.N, 1).then_inc(iota_done, 1)
            nc.gpsimd.iota(int_c[:, o + 1:o + 2], [[0, 1]], (127 + 63) << 23, -(1 << 23)).then_inc(iota_done, 1)
            nc.gpsimd.iota(int_c[:, o + 2:o + 3], [[0, 1]], ((127 + 64) << 23) + (1 << 21), -(1 << 23)).then_inc(iota_done, 1)
            pool.wait_ge(const_set, 4)
            nc.gpsimd.affine_select(out=g.identF[:, :], in_=g.identF[:, :], compare_op=ALU.not_equal, fill=1.0,
                                    base=0, pattern=[[-1, P]], channel_multiplier=1).then_inc(const_sel, 1)
            nc.gpsimd.affine_select(out=g.identB[:, :], in_=g.identB[:, :], compare_op=ALU.not_equal, fill=1.0,
                                    base=0, pattern=[[-1, P]], channel_multiplier=1).then_inc(const_sel, 1)
            nc.gpsimd.affine_select(out=g.sel[:, :, :], in_=g.sel[:, :, :], compare_op=ALU.not_equal, fill=128.0,
                                    base=0, pattern=[[-1, CT], [0, P]], channel_multiplier=1).then_inc(const_sel, 1)
            pool.wait_ge(const_sel, 3)
            nc.gpsimd.affine_select(out=g.sel[:, :, :], in_=g.sel[:, :, :], compare_op=ALU.not_equal, fill=1.0,
                                    base=-CT, pattern=[[-1, CT], [0, P]], channel_multiplier=1).then_inc(const_sel, 1)
            pool.wait_ge(zeroed, 1)
            pool.dma_start(flat(g.acc[0][0:g.N, :]), flat(ins["x"])).then_inc(g.acc_done[0], 16)
            for k in range(1, ACCS):
                pool.dma_start(g.acc[k].rearrange("(p t) d -> p (t d)", p=P), g.zeros[:, :]).then_inc(g.acc_done[k], 16)

        @block.vector
        def _(dve):
            steps = [0]

            def then(ins_):
                steps[0] += 1
                ins_.then_inc(v_step, 1)
                dve.wait_ge(v_step, steps[0])

            nc.vector.memset(g.xres[96:P, :], 0.0)
            dve.wait_ge(dst_in, 16)
            then(nc.vector.tensor_copy(g.dstF[:, :, :], idx_i[:, 1, :, :]))
            nc.vector.tensor_reduce(ext[:, 0, :], g.dstF[:, :, :], AX_X, ALU.min).then_inc(ext_ready, 1)
            nc.vector.tensor_reduce(ext[:, 1, :], g.dstF[:, :, :], AX_X, ALU.max).then_inc(ext_ready, 1)
            dve.wait_ge(src_in, 16)
            nc.vector.tensor_single_scalar(idx_i[:, 1, :, :], idx_i[:, 0, :, :], 7,
                                           ALU.arith_shift_right).then_inc(digit_ready, 1)
            nc.vector.tensor_single_scalar(digit[:, :, :], idx_i[:, 0, :, :], 127, ALU.bitwise_and).then_inc(digit_ready, 1)
            dve.wait_ge(ext_turned, 1)
            nc.vector.tensor_reduce(colx[0:g.NC, 0:1], ps_t[0:g.NC, 0, 0:P], AX_X, ALU.min)
            then(nc.vector.tensor_reduce(colx[0:g.NC, 1:2], ps_t[0:g.NC, 1, 0:P], AX_X, ALU.max))
            then(nc.vector.tensor_copy(colb[0:g.NC, :, :], bcast(colx[0:g.NC, :], 2, P)))
            nc.vector.tensor_copy(colb[0:g.NC, 0, 0:1], colx[0:g.NC, 0:1]).then_inc(col_ready, 1)
            dve.wait_ge(ext_spread, 1)
            nc.vector.tensor_copy(g.minB[:, :], ps_t[:, 0, 0:g.NC])
            nc.vector.tensor_copy(g.tab_min[:, :], ps_t[:, 0, 0:g.NC])
            then(nc.vector.tensor_copy(g.tab_nw[:, :], ps_t[:, 1, 0:g.NC]))
            then(nc.vector.tensor_tensor(g.tab_nw[:, :], g.tab_nw[:, :], g.tab_min[:, :], ALU.subtract))
            then(nc.vector.tensor_single_scalar(g.tab_nw[:, :], g.tab_nw[:, :], 7, ALU.arith_shift_right))
            nc.vector.tensor_single_scalar(g.tab_nw[:, :], g.tab_nw[:, :], 1, ALU.add)
            o = WIN + g.NW
            dve.wait_ge(iota_done, 5)
            nc.vector.tensor_copy(g.iota_w[:, :], int_c[:, 0:WIN])
            nc.vector.tensor_copy(g.win_off[:, :], int_c[:, WIN:o])
            nc.vector.tensor_copy(g.trash[:, :], int_c[:, o:o + 1])
            nc.vector.tensor_copy(g.pow_col[:, :], int_c[:, o + 1:o + 2].bitcast(F32))
            nc.vector.tensor_copy(g.pow_lim[:, :], int_c[:, o + 2:o + 3].bitcast(F32))
            dve.wait_ge(w_turned, 1)
            nc.vector.tensor_scalar_mul(g.Wc1T[:, :], ps_w[:, 1, 0:g.D], 0.5)
            for k in range(2):
                lo = slice(k * g.D, (k + 1) * g.D)
                for to, i, factor in ((g.V1d, 0, 1.0), (g.Wc2d, 2, 2.0), (g.V2d, 3, 0.5), (g.V3d, 4, 2.0)):
                    nc.vector.memset(to[lo, 1 - k, :], 0.0)
                    nc.vector.tensor_scalar_mul(to[lo, k, :], ps_w[lo, i, 0:g.D], factor)
            nc.vector.tensor_scalar_mul(g.bc1h[:, :], g.bc1h[:, :], 0.5)
            nc.vector.tensor_scalar_mul(g.v2h[:, :], g.v2h[:, :], 0.5)
            dve.wait_ge(bias_in, 48)
            for k, ins_ in enumerate(split_steps(nc, [bias_part[:, k] for k in range(3)],
                                                 [bias_left[:, k] for k in range(2)], bias[:, :, :])):
                if k < 4:
                    then(ins_())
                else:
                    ins_().then_inc(bias_split, 1)

        @block.tensor
        def _(pe):
            pe.wait_ge(const_sel, 4)
            pe.wait_ge(ext_ready, 2)
            nc.tensor.transpose(ps_t[0:g.NC, 0, 0:P], ext[:, 0, :], g.identF[:, :])
            nc.tensor.transpose(ps_t[0:g.NC, 1, 0:P], ext[:, 1, :], g.identF[:, :]).then_inc(ext_turned, 1)
            pe.wait_ge(col_ready, 1)
            for i in range(2):
                last = nc.tensor.matmul(ps_t[:, i, 0:g.NC], colb[0:g.NC, i, :], g.identF[0:g.NC, 0:g.NC],
                                        start=True, stop=True)
            last.then_inc(ext_spread, 1)
            pe.wait_ge(w_in, 16 * 17)
            for i in range(5):
                last = nc.tensor.transpose(ps_w[:, i, 0:g.D], wload[:, i, :], g.identF[0:g.D, 0:g.D])
            last.then_inc(w_turned, 1)


def each_unit(eng, g, name):
    done = eng.alloc_register(name)
    eng.reg_mov(done, 0)
    with eng.Fori(0, g.NC) as c:
        windows = eng.value_load(g.tab_nw[0:1, bass.ds(c, 1)], min_val=1, max_val=g.NW)
        with eng.Fori(0, windows) as w:
            yield c, w, eng.snap(done, min_val=0, max_val=g.NC * g.NW)
            eng.reg_add(done, done, 1)
    yield None, None, eng.snap(done, min_val=0, max_val=g.NC * g.NW)


def window_base(eng, g, c, w, name):
    first = eng.value_load(g.tab_min[0:1, bass.ds(c, 1)], min_val=0, max_val=g.N - 1)
    base = eng.alloc_register(name)
    eng.reg_mov(base, first + w * WIN)
    return eng.snap(base, min_val=0, max_val=g.N - 1)


def layer0_edges(nc, g):
    with ExitStack() as ctx:
        def sb(name, shape, dt):
            return ctx.enter_context(nc.sbuf_tensor(name, shape, dt))

        def ps(name, shape, dt):
            return ctx.enter_context(nc.psum_tensor(name, shape, dt))

        def sem(name):
            return ctx.enter_context(nc.semaphore(name))

        x_win = sb("x_win", [WIN, g.D], F32)
        x_part = sb("x_part", [WIN, 3, g.D], BF16)
        x_left = sb("x_left", [WIN, 2, g.D], F32)
        cur_hl = sb("cur_hl", [P, 2 * CT], BF16)
        cur_src = sb("cur_src", [P, CT], F32)
        cur_dst = sb("cur_dst", [P, CT], F32)
        to_trash = sb("to_trash", [P, CT], F32)
        src_rows = sb("src_rows", [2 * CT, P], BF16)
        oh = sb("oh", [P, CT, WIN], BF16)
        eq = sb("eq", [P, CT, P], BF16)
        counts = sb("counts", [WIN, GT, P], BF16)
        moved = sb("moved", [P, CT], F32)
        target = sb("target", [P, CT], I32)
        rows = sb("rows", [P, CT, g.D], F32)
        ps_hl = ps("ps_hl", [2 * CT, P], BF16)
        ps_src = ps("ps_src", [P, 2 * BANK], F32)
        ps_cnt = ps("ps_cnt", [P, 2 * BANK], F32)
        ps_first = ps("ps_first", [P, BANK], F32)
        ps_rows = ps("ps_rows", [P, BANK], F32)
        spread = ps_src[:, 0:GT * P].rearrange("p (t e) -> p t e", t=GT)
        cnt = ps_cnt[:, 0:GT * P].rearrange("p (t e) -> p t e", t=GT)
        sums = ps_rows[:, 0:GT * g.D].rearrange("p (t d) -> p t d", t=GT)

        x_win_in = sem("x_win_in")
        split_step = sem("split_step")
        x_in = sem("x_in")
        cur_ready = sem("cur_ready")
        hl_turned = sem("hl_turned")
        hl_copied = sem("hl_copied")
        spread_done = sem("spread_done")
        eq_ready = sem("eq_ready")
        cnt_done = sem("cnt_done")
        cnt_copied = sem("cnt_copied")
        sums_done = sem("sums_done")
        rows_ready = sem("rows_ready")
        mark_ready = sem("mark_ready")
        target_ready = sem("target_ready")
        rows_free = sem("rows_free")

        block = ctx.enter_context(nc.Block())

        @block.sync
        def _(sp):
            for c, w, u in each_unit(sp, g, "sp_unit"):
                if c is None:
                    continue
                base = window_base(sp, g, c, w, "sp_base")
                sp.wait_ge(split_step, u * SPLIT + SPLIT)
                sp.dma_start(x_win[:, :], g.xp[bass.ds(base, WIN), :]).then_inc(x_win_in, 16)
            load_nodes(sp, g, g.xres, g.ins["x"], x_in)
            sp.wait_ge(x_in, 48)

        @block.vector
        def _(dve):
            def one_hot(j):
                t = slice(j * GT, (j + 1) * GT)
                return nc.vector.tensor_tensor(oh[:, t, :], bcast(g.iota_w[:, :], 1, GT),
                                               bcast(cur_dst[:, t], 2, WIN), ALU.is_equal)

            dve.sem_inc(target_ready, 1)
            dve.sem_inc(split_step, SPLIT)
            split = split_steps(nc, [x_part[:, k, :] for k in range(3)], [x_left[:, k, :] for k in range(2)], x_win[:, :])
            for c, w, u in each_unit(dve, g, "dve_unit"):
                if c is None:
                    continue
                G = dve.snap(u * GR)
                dve.wait_ge(target_ready, G + 1)
                nc.vector.tensor_copy(cur_hl[:, :], g.src_hl[:, bass.ds(c, 1), :].rearrange("p a t -> p (a t)"))
                src_c = g.srcF[:, bass.ds(c, 1), :].rearrange("p a t -> p (a t)")
                dst_c = g.dstF[:, bass.ds(c, 1), :].rearrange("p a t -> p (a t)")
                nc.vector.tensor_copy(cur_src[:, :], src_c)
                nc.vector.tensor_scalar(to_trash[:, :], src_c, -1.0, g.trash[:, 0:1], ALU.mult, ALU.add)
                nc.vector.tensor_scalar(cur_dst[:, :], dst_c, g.minB[:, bass.ds(c, 1)],
                                        g.win_off[:, bass.ds(w, 1)], ALU.subtract, ALU.subtract).then_inc(cur_ready, 1)
                dve.wait_ge(cur_ready, u + 1)
                one_hot(0)
                for j in range(GR):
                    t = slice(j * GT, (j + 1) * GT)
                    dve.wait_ge(spread_done, G + (j + 1))
                    nc.vector.tensor_tensor(eq[:, t, :], spread, bcast(cur_src[:, t], 2, P),
                                            ALU.is_equal).then_inc(eq_ready, 1)
                    if j == 0:
                        dve.wait_ge(x_win_in, u * 16 + 16)
                        dve.wait_ge(sums_done, u * GR + GR)
                        for k in range(SPLIT):
                            dve.wait_ge(split_step, u * SPLIT + (SPLIT + k))
                            split[k]().then_inc(split_step, 1)
                    if j + 1 < GR:
                        one_hot(j + 1)
                    dve.wait_ge(cnt_done, G + (j + 1))
                    nc.vector.scalar_tensor_tensor(out=moved[:, t], in0=ps_first[:, t], scalar=g.pow_lim[:, 0:1],
                                                   in1=to_trash[:, t], op0=ALU.is_gt, op1=ALU.mult).then_inc(mark_ready, 1)
                    dve.wait_ge(mark_ready, G + (j + 1))
                    dve.wait_ge(rows_free, G + (j + 1))
                    nc.vector.tensor_tensor(target[:, t], moved[:, t], cur_src[:, t], ALU.add).then_inc(target_ready, 1)

        @block.scalar
        def _(act):
            act.sem_inc(rows_ready, 1)
            for c, w, u in each_unit(act, g, "act_unit"):
                if c is None:
                    continue
                G = act.snap(u * GR)
                act.wait_ge(hl_turned, u + 1)
                nc.scalar.copy(src_rows[:, :], ps_hl[:, :]).then_inc(hl_copied, 1)
                for j in range(GR):
                    t = slice(j * GT, (j + 1) * GT)
                    act.wait_ge(cnt_done, G + (j + 1))
                    nc.scalar.copy(counts[:, :, :], cnt).then_inc(cnt_copied, 1)
                    act.wait_ge(sums_done, G + (j + 1 + GR))
                    act.wait_ge(rows_free, G + (j + 1))
                    nc.scalar.copy(rows[:, t, :], sums).then_inc(rows_ready, 1)

        @block.tensor
        def _(pe):
            def spread_group(j):
                for i in range(GT):
                    last = nc.tensor.matmul(spread[:, i, :], g.sel[:, j * GT + i, :], src_rows[:, :],
                                            start=True, stop=True)
                last.then_inc(spread_done, 1)

            pe.sem_inc(sums_done, GR)
            for c, w, u in each_unit(pe, g, "pe_unit"):
                if c is None:
                    continue
                G = pe.snap(u * GR)
                wait_alone(pe, cur_ready, u + 1, g.pe_turn)
                nc.tensor.transpose(ps_hl[:, :], cur_hl[:, :], g.identB[:, :]).then_inc(hl_turned, 1)
                pe.wait_ge(hl_copied, u + 1)
                spread_group(0)
                for j in range(GR):
                    pe.wait_ge(eq_ready, G + (j + 1))
                    for i in range(GT):
                        nc.tensor.matmul(cnt[:, i, :], oh[:, j * GT + i, :], eq[:, j * GT + i, :],
                                         start=True, stop=True)
                    for i in range(GT):
                        s = j * GT + i
                        last = nc.tensor.matmul(ps_first[:, s:s + 1], eq[:, s, :], g.pow_col[:, :],
                                                start=True, stop=True)
                    last.then_inc(cnt_done, 1)
                    if j + 1 < GR:
                        spread_group(j + 1)
                    pe.wait_ge(cnt_copied, G + (j + 1))
                    if j == 0:
                        pe.wait_ge(split_step, u * SPLIT + 2 * SPLIT)
                    pe.wait_ge(rows_ready, G + (j + 1))
                    for i in range(GT):
                        for part in range(3):
                            last = nc.tensor.matmul(sums[:, i, :], counts[:, i, :], x_part[:, part, :],
                                                    start=(part == 0), stop=(part == 2))
                    last.then_inc(sums_done, 1)

        @block.gpsimd
        def _(pool):
            pool.sem_inc(rows_free, GR - 1)
            for c, w, u in each_unit(pool, g, "pool_unit"):
                G = pool.snap(u * GR)
                if c is None:
                    for k in range(ACCS):
                        pool.wait_ge(g.acc_done[k], G * 16 + 16)
                    continue
                for j in range(GR):
                    pool.wait_ge(rows_ready, G + (j + 2))
                    pool.wait_ge(target_ready, G + (j + 2))
                    before = pool.snap(G * 16 + 16 * (j + 1))
                    for i in range(GT):
                        s = j * GT + i
                        wait_alone(pool, g.acc_done[i], before, g.pool_turn)
                        pool.indirect_dma_start(g.acc[i][:, :], bass.IndirectOffsetOnAxis(target[:, s:s + 1], 0),
                                                rows[:, s, :], None, compute_op=ALU.add).then_inc(g.acc_done[i], 16)
                    pool.sem_inc(rows_free, 1)


def layer_norm(nc, g, r, d, sq, stat, out):
    return (lambda: nc.vector.tensor_reduce(stat[:, 0, :], r, AX_X, ALU.add),
            lambda: nc.vector.tensor_scalar_mul(stat[:, 1, :], stat[:, 0, :], 1.0 / g.D),
            lambda: nc.vector.tensor_tensor(d, r, bcast(stat[:, 1, :], 2, g.D), ALU.subtract),
            lambda: nc.vector.tensor_tensor(sq, d, d, ALU.mult),
            lambda: nc.vector.tensor_reduce(stat[:, 2, :], sq, AX_X, ALU.add),
            lambda: nc.vector.tensor_scalar(stat[:, 3, :], stat[:, 2, :], 1.0 / g.D, EPS, ALU.mult, ALU.add),
            lambda: nc.vector.reciprocal(stat[:, 5, :], stat[:, 4, :]),
            lambda: nc.vector.tensor_tensor(out, d, bcast(stat[:, 5, :], 2, g.D), ALU.mult))


LN_STEPS = 8
LN_SQRT = 6


def node_phase0(nc, g):
    PAIRS = g.NB // 2
    L = range(2)
    T = LANE_TILES
    C = [t * g.D for t in T]
    AT = [t * g.D for t in LANE_AT]
    ALL = sum(C)
    assert ACCS == 5 and 2 * g.D == P and max(C) <= BANK
    with ExitStack() as ctx:
        def sb(name, shape, dt=F32):
            return [ctx.enter_context(nc.sbuf_tensor(f"{name}{h}", shape(h), dt)) for h in L]

        def ps(name, shape):
            return [ctx.enter_context(nc.psum_tensor(f"{name}{h}", shape, F32)) for h in L]

        def sem(name):
            return [ctx.enter_context(nc.semaphore(f"{name}{h}")) for h in L]

        def cols(h):
            return [P, C[h]]

        def tiles(h):
            return [P, T[h], g.D]

        parts = sb("agg_in_sb", lambda h: [P, ACCS, C[h]])
        total = sb("total", cols)
        sT = sb("sT", cols)
        hT = sb("hT", lambda h: [g.HID, 2, C[h]])
        r = sb("r0", tiles)
        d = sb("d0", tiles)
        sq = sb("sq0", tiles)
        stat = sb("stat0", lambda h: [P, 6, T[h]])
        x1 = sb("x1", tiles)
        x1T = sb("x1T", cols)
        nn = sb("nn", cols)
        ps_s = ps("ps_s", [P, BANK])
        ps_x = ps("ps_x", [P, BANK])
        ps_p = ps("ps_prod", [P, 2, BANK])

        agg_in = sem("agg_in")
        paired = sem("paired")
        added = sem("added")
        s_turned = sem("s_turned")
        s_copied = sem("s_copied")
        h_done = sem("h_done")
        relu_done = sem("relu_done")
        y_done = sem("y_done")
        r_ready = sem("r_ready")
        ln_step = sem("ln_step0")
        std_ready = sem("std_ready0")
        x1_turned = sem("x1_turned")
        x1_copied = sem("x1_copied")
        x1_kept = sem("x1_kept")
        nn_done = sem("nn_done")
        nn_copied = sem("nn_copied")
        nn_out = sem("nn_out")
        cf_zero = ctx.enter_context(nc.semaphore("cf_zero"))

        acc_v = [a[0:P * g.NT, :].rearrange("(p t) d -> p (t d)", t=g.NT) for a in g.acc]
        nn_v = g.nn[0:P * g.NT, :].rearrange("(p t) d -> p (t d)", t=g.NT)
        block = ctx.enter_context(nc.Block())

        @block.sync
        def _(sp):
            for h in L:
                for k in range(ACCS):
                    sp.dma_start(parts[h][:, k, :], acc_v[k][:, AT[h]:AT[h] + C[h]]).then_inc(agg_in[h], 16)
            with sp.Fori(0, PAIRS - 1) as v:
                for h in L:
                    sp.wait_ge(added[h], v * 2 + 2)
                    for k in range(ACCS):
                        sp.dma_start(parts[h][:, k, :], acc_v[k][:, bass.ds(v * ALL + (ALL + AT[h]), C[h])]).then_inc(agg_in[h], 16)
            sp.dma_start(g.cf.rearrange("(p t) d -> p (t d)", p=P), g.zeros[:, :]).then_inc(cf_zero, 16)
            sp.wait_ge(cf_zero, 16)

        @block.gpsimd
        def _(pool):
            with pool.Fori(0, PAIRS) as v:
                for k in (1, 3):
                    for h in L:
                        pool.wait_ge(agg_in[h], (v + 1) * (16 * ACCS))
                        nc.gpsimd.tensor_tensor(parts[h][:, k, :], parts[h][:, k, :], parts[h][:, k + 1, :],
                                                ALU.add).then_inc(paired[h], 1)

        @block.vector
        def _(dve):
            def x_cols(v):
                return [g.xres[:, bass.ds(held(dve, v * ALL + AT[h]), C[h])] for h in L]

            def add_up(v):
                for h in L:
                    dve.wait_ge(agg_in[h], (v + 1) * (16 * ACCS))
                    dve.wait_ge(paired[h], v * 2 + 1)
                    dve.wait_ge(s_turned[h], v + 1)
                    nc.vector.tensor_tensor(total[h][:, :], parts[h][:, 0, :], parts[h][:, 1, :],
                                            ALU.add).then_inc(added[h], 1)
                for h in L:
                    dve.wait_ge(paired[h], v * 2 + 2)
                    dve.wait_ge(added[h], v * 2 + 1)
                    nc.vector.tensor_tensor(total[h][:, :], total[h][:, :], parts[h][:, 3, :],
                                            ALU.add).then_inc(added[h], 1)

            def residual(v):
                x = x_cols(v)
                for h in L:
                    dve.wait_ge(y_done[h], v + 1)
                    dve.wait_ge(ln_step[h], v * LN_STEPS + 1)
                    nc.vector.tensor_tensor(r[h][:, :, :].rearrange("p t d -> p (t d)"), ps_p[h][:, 0, 0:C[h]], x[h],
                                            ALU.add).then_inc(r_ready[h], 1)

            def normalise(v):
                steps = [layer_norm(nc, g, r[h][:, :, :], d[h][:, :, :], sq[h][:, :, :], stat[h], x1[h][:, :, :])
                         for h in L]
                for k in range(LN_STEPS):
                    for h in L:
                        if k == 0:
                            dve.wait_ge(r_ready[h], v + 2)
                        elif k == LN_SQRT:
                            dve.wait_ge(std_ready[h], v + 1)
                        else:
                            dve.wait_ge(ln_step[h], v * LN_STEPS + (k + 1))
                        if k == LN_STEPS - 1:
                            dve.wait_ge(x1_kept[h], v + 1)
                            dve.wait_ge(x1_turned[h], v + 1)
                        steps[h][k]().then_inc(ln_step[h], 1)

            for h in L:
                dve.sem_inc(ln_step[h], 1)
                dve.sem_inc(r_ready[h], 1)
            add_up(0)
            add_up(1)
            residual(0)
            with dve.Fori(0, PAIRS - 2) as v:
                add_up(v + 2)
                normalise(v)
                residual(v + 1)
            normalise(PAIRS - 2)
            residual(PAIRS - 1)
            normalise(PAIRS - 1)

        @block.scalar
        def _(act):
            def copy_s(v):
                for h in L:
                    act.wait_ge(s_turned[h], v + 2)
                    nc.scalar.copy(sT[h][:, :], ps_s[h][:, 0:C[h]]).then_inc(s_copied[h], 1)

            def root(v):
                for h in L:
                    act.wait_ge(ln_step[h], v * LN_STEPS + (LN_SQRT + 1))
                    nc.scalar.sqrt(stat[h][:, 4, :], stat[h][:, 3, :]).then_inc(std_ready[h], 1)

            def relu(v):
                for h in L:
                    act.wait_ge(h_done[h], v + 1)
                    nc.scalar.activation(hT[h][:, :, :], ps_p[h][:, :, 0:C[h]], ACT.Relu,
                                         bias=g.b1[:, 0:1]).then_inc(relu_done[h], 1)

            def keep_and_store(v):
                col = [held(act, v * ALL + AT[h]) for h in L]
                for h in L:
                    act.wait_ge(ln_step[h], v * LN_STEPS + (LN_STEPS + 1))
                    nc.scalar.copy(g.xres[:, bass.ds(col[h], C[h])],
                                   x1[h][:, :, :].rearrange("p t d -> p (t d)")).then_inc(x1_kept[h], 1)
                for h in L:
                    act.wait_ge(x1_turned[h], v + 2)
                    nc.scalar.copy(x1T[h][:, :], ps_x[h][:, 0:C[h]]).then_inc(x1_copied[h], 1)
                for h in L:
                    act.wait_ge(nn_done[h], v + 1)
                    act.wait_ge(nn_out[h], (v + 1) * 16)
                    nc.scalar.copy(nn[h][:, :], ps_p[h][:, 1, 0:C[h]]).then_inc(nn_copied[h], 1)
                for h in L:
                    act.wait_ge(nn_copied[h], v + 3)
                    act.dma_start(nn_v[:, bass.ds(col[h], C[h])], nn[h][:, :]).then_inc(nn_out[h], 16)

            for h in L:
                act.sem_inc(nn_out[h], 16)
                act.sem_inc(nn_copied[h], 2)
                act.sem_inc(x1_kept[h], 1)
            act.preload_act_table_set("sqrt_and_others")
            copy_s(0)
            relu(0)
            copy_s(1)
            with act.Fori(0, PAIRS - 2) as v:
                relu(v + 1)
                copy_s(v + 2)
                root(v)
                keep_and_store(v)
            relu(PAIRS - 1)
            root(PAIRS - 2)
            keep_and_store(PAIRS - 2)
            root(PAIRS - 1)
            keep_and_store(PAIRS - 1)
            for h in L:
                act.wait_ge(nn_out[h], 16 * (PAIRS + 1))

        @block.tensor
        def _(pe):
            def turn(v):
                for h in L:
                    pe.wait_ge(added[h], v * 2 + 2)
                    pe.wait_ge(s_copied[h], v + 1)
                    for k in range(T[h] // 2):
                        two = slice(k * P, (k + 1) * P)
                        last = nc.tensor.transpose(ps_s[h][:, two], total[h][:, two], g.identF[:, :])
                    last.then_inc(s_turned[h], 1)

            def first_product(v):
                for h in L:
                    pe.wait_ge(nn_copied[h], v + 1)
                    pe.wait_ge(r_ready[h], v + 1)
                    wait_alone(pe, s_copied[h], v + 2, g.pe_turn)
                    for k in range(2):
                        half = slice(k * g.D, (k + 1) * g.D)
                        last = nc.tensor.matmul(ps_p[h][:, k, 0:C[h]], g.W1[half, :], sT[h][half, :],
                                                start=True, stop=True)
                    last.then_inc(h_done[h], 1)

            def second_product(v):
                for h in L:
                    y = ps_p[h][:, 0, 0:C[h]]
                    pe.wait_ge(relu_done[h], v + 1)
                    nc.tensor.matmul(y, g.ones3[:, :], g.b2p[:, 0:T[h], :].rearrange("o t d -> o (t d)"),
                                     start=True, stop=False, skip_group_check=True)
                    for t in range(T[h]):
                        last = nc.tensor.matmul(y[:, t * g.D:(t + 1) * g.D],
                                                hT[h][:, t % 2, t // 2 * P:(t // 2 + 1) * P], g.W2[:, :],
                                                start=False, stop=(t == T[h] - 1), skip_group_check=True)
                    last.then_inc(y_done[h], 1)

            def new_node(v):
                for h in L:
                    pe.wait_ge(ln_step[h], v * LN_STEPS + (LN_STEPS + 1))
                    for k in range(T[h] // 2):
                        last = nc.tensor.transpose(ps_x[h][:, k * P:(k + 1) * P],
                                                   x1[h][:, 2 * k:2 * k + 2, :].rearrange("p t d -> p (t d)"),
                                                   g.identF[:, :])
                    last.then_inc(x1_turned[h], 1)
                for h in L:
                    pe.wait_ge(x1_copied[h], v + 1)
                    for k in range(T[h] // 2):
                        two = slice(k * P, (k + 1) * P)
                        last = nc.tensor.matmul(ps_p[h][:, 1, two], x1T[h][:, two],
                                                g.V1d[:, :, :].rearrange("p a d -> p (a d)"), start=True, stop=True)
                    last.then_inc(nn_done[h], 1)

            for h in L:
                pe.sem_inc(s_turned[h], 1)
                pe.sem_inc(s_copied[h], 1)
                pe.sem_inc(x1_turned[h], 1)
            turn(0)
            first_product(0)
            turn(1)
            second_product(0)
            with pe.Fori(0, PAIRS - 2) as v:
                first_product(v + 1)
                turn(v + 2)
                second_product(v + 1)
                new_node(v)
            first_product(PAIRS - 1)
            second_product(PAIRS - 1)
            new_node(PAIRS - 2)
            new_node(PAIRS - 1)


def layer1_edges(nc, g):
    HALF = GT * P // 2
    MID = GT // 2
    ZB = 3
    with ExitStack() as ctx:
        def sb(name, shape, dt=F32):
            return ctx.enter_context(nc.sbuf_tensor(name, shape, dt))

        def ps(name, shape):
            return ctx.enter_context(nc.psum_tensor(name, shape, F32))

        def sem(name):
            return ctx.enter_context(nc.semaphore(name))

        ea = sb("ea", [P, CT, g.F])
        ea_T = sb("ea_T", [g.F, 2, HALF])
        cur_dst = sb("cur_dst1", [P, CT])
        oh = sb("oh1", [P, CT, WIN])
        y_cap = sb("y_cap", [P, HALF])
        e_y = sb("e_y", [P, HALF])
        q = sb("q", [P, HALF])
        sp_y = sb("sp_y", [P, GR, HALF])
        idx = sb("idx", [P, CT], I32)
        nn = sb("nn_rows", [P, CT, g.D])
        msg = sb("msg", [P, CT, g.D])
        seg = sb("seg", [WIN, g.D])
        cf_old = sb("cf_old", [WIN, g.D])
        ps_t = ps("ps_t", [P, 2, BANK])
        ps_z = ps("ps_z", [P, ZB, BANK])
        ps_e = ps("ps_e", [P, 2, BANK])
        ps_seg = ps("ps_seg", [P, BANK])

        ea_in = [sem(f"ea_in{j}") for j in range(GR)]
        idx_in = [sem(f"idx_in{j}") for j in range(GR)]
        gathered = [sem(f"gathered{j}") for j in range(GR)]
        turned = sem("turned")
        turn_copied = sem("turn_copied")
        z_done = sem("z_done")
        capped = sem("capped")
        exp_done = sem("exp_done")
        log_done = sem("log_done")
        sp_ready = sem("sp_ready")
        h_done = sem("h_done1")
        msg_ready = sem("msg_ready")
        dst_ready = sem("dst_ready")
        seg_group = sem("seg_group")
        seg_ready = sem("seg_ready")
        cf_in = sem("cf_old_in")
        cf_out = sem("cf_out")

        src_v = g.ins["src"].rearrange("(c p t) -> p c t", p=P, t=CT)
        ea_v = g.ins["edge_attr_128"].rearrange("(c p t) f -> c p (t f)", p=P, t=CT)
        block = ctx.enter_context(nc.Block())

        @block.sync
        def _(sp):
            def load_attributes(c, j, G):
                sp.wait_ge(turned, G + (j + 1))
                sp.dma_start(ea[:, j * GT:(j + 1) * GT, :].rearrange("p t f -> p (t f)"),
                             ea_v[bass.ds(c, 1), :, j * GT * g.F:(j + 1) * GT * g.F].rearrange("a p f -> (a p) f")
                             ).then_inc(ea_in[j], 16)

            last_base = sp.alloc_register("last_base")
            sp.reg_mov(last_base, 0)

            def store_window(u):
                sp.wait_ge(seg_ready, u + 1)
                last = sp.snap(last_base, min_val=0, max_val=g.N - 1)
                sp.dma_start(g.cf[bass.ds(last, WIN), :], seg[:, :]).then_inc(cf_out, 16)
                wait_alone(sp, cf_out, u * 16 + 16, g.sp_turn)

            for c, w, u in each_unit(sp, g, "sp_unit1"):
                G = sp.snap(u * GR)
                if c is None:
                    for j in range(2):
                        load_attributes(0, j, G)
                    store_window(u)
                    continue
                base = window_base(sp, g, c, w, "sp_base1")
                for j in range(GR):
                    load_attributes(c, j, G)
                    sp.wait_ge(msg_ready, G + (j + 1))
                    with nc.allow_non_contiguous_dma("five indices a partition"):
                        sp.dma_start(idx[:, j * GT:(j + 1) * GT],
                                     src_v[:, bass.ds(c, 1), j * GT:(j + 1) * GT].rearrange("p a t -> p (a t)")
                                     ).then_inc(idx_in[j], 16)
                store_window(u)
                sp.dma_start(cf_old[:, :], g.cf[bass.ds(base, WIN), :]).then_inc(cf_in, 16)
                sp.reg_mov(last_base, base)

        @block.gpsimd
        def _(pool):
            for c, w, u in each_unit(pool, g, "pool_unit1"):
                if c is None:
                    continue
                G = pool.snap(u * GR)
                for j in range(GR):
                    pool.wait_ge(idx_in[j], u * 16 + 16)
                    wait_alone(pool, msg_ready, G + (j + 1), g.pool_turn)
                    for i in range(GT):
                        s = j * GT + i
                        pool.indirect_dma_start(nn[:, s, :], None, g.nn[0:g.N, :],
                                                bass.IndirectOffsetOnAxis(idx[:, s:s + 1], 0)).then_inc(gathered[j], 16)

        @block.vector
        def _(dve):
            def message(j, G, u):
                t = slice(j * GT, (j + 1) * GT)
                dve.wait_ge(h_done, G + (j + 1))
                dve.wait_ge(gathered[j], u * (16 * GT) + 16 * GT)
                nc.vector.tensor_tensor(msg[:, t, :], ps_e[:, j % 2, 0:GT * g.D].rearrange("p (t d) -> p t d", d=g.D),
                                        nn[:, t, :], ALU.mult).then_inc(msg_ready, 1)

            def cap(j, G):
                dve.wait_ge(z_done, G + (j + 1))
                nc.vector.tensor_scalar(y_cap[:, :], ps_z[:, j % GR % ZB, 0:HALF], g.bc1h[:, 0:1], CAP,
                                        ALU.add, ALU.min).then_inc(capped, 1)

            def softplus(j, G):
                dve.wait_ge(log_done, G + (j + 1))
                nc.vector.scalar_tensor_tensor(out=sp_y[:, j % GR, :], in0=ps_z[:, j % GR % ZB, 0:HALF],
                                               scalar=g.bc1h[:, 0:1], in1=q[:, :],
                                               op0=ALU.add, op1=ALU.max).then_inc(sp_ready, 1)

            dve.sem_inc(msg_ready, GR)
            nc.vector.memset(seg[:, :], 0.0).then_inc(seg_ready, 1)
            cap(0, 0)
            softplus(0, 0)
            for c, w, u in each_unit(dve, g, "dve_unit1"):
                if c is None:
                    continue
                G = dve.snap(u * GR)
                dst_c = g.dstF[:, bass.ds(c, 1), :].rearrange("p a t -> p (a t)")
                dve.wait_ge(msg_ready, G + GR)
                nc.vector.tensor_scalar(cur_dst[:, :], dst_c, g.minB[:, bass.ds(c, 1)],
                                        g.win_off[:, bass.ds(w, 1)], ALU.subtract, ALU.subtract).then_inc(dst_ready, 1)
                for j in range(GR):
                    t = slice(j * GT, (j + 1) * GT)
                    cap(j + 1, G)
                    if j == 0:
                        dve.wait_ge(dst_ready, u + 1)
                    else:
                        message(j - 1, G, u)
                    dve.wait_ge(seg_group, G + (j + 1))
                    nc.vector.tensor_tensor(oh[:, t, :], bcast(g.iota_w[:, :], 1, GT),
                                            bcast(cur_dst[:, t], 2, WIN), ALU.is_equal)
                    softplus(j + 1, G)
                message(GR - 1, G, u)
                dve.wait_ge(seg_group, G + 2 * GR)
                dve.wait_ge(cf_in, u * 16 + 16)
                nc.vector.tensor_tensor(seg[:, :], ps_seg[:, 0:g.D], cf_old[:, :], ALU.add).then_inc(seg_ready, 1)

        @block.scalar
        def _(act):
            def copy_turned(j, G):
                act.wait_ge(turned, G + (j + 1 + GR))
                nc.scalar.copy(ea_T[:, :, :], ps_t[:, :, 0:HALF]).then_inc(turn_copied, 1)

            def logarithm(j, G):
                act.wait_ge(capped, G + (j + 1))
                nc.scalar.activation(e_y[:, :], y_cap[:, :], ACT.Exp).then_inc(exp_done, 1)
                act.wait_ge(exp_done, G + (j + 1))
                nc.scalar.activation(q[:, :], e_y[:, :], ACT.Ln, bias=1.0).then_inc(log_done, 1)

            act.preload_act_table_set("natural_log_exp_and_others")
            copy_turned(0, 0)
            logarithm(0, 0)
            copy_turned(1, 0)
            for c, w, u in each_unit(act, g, "act_unit1"):
                if c is None:
                    continue
                G = act.snap(u * GR)
                for j in range(GR):
                    logarithm(j + 1, G)
                    copy_turned(j + 2, G)

        @block.tensor
        def _(pe):
            def turn(j, G, rounds):
                pe.wait_ge(ea_in[j % GR], rounds)
                for bank, at, i in ((1, HALF - P, MID), (0, 0, 0), (0, P, 1), (0, 2 * P, MID), (1, 0, 3), (1, P, 4)):
                    last = nc.tensor.transpose(ps_t[:, bank, at:at + P], ea[:, j % GR * GT + i, :], g.identF[:, :])
                last.then_inc(turned, 1)

            def first(j, G):
                pe.wait_ge(turn_copied, G + (j + 1))
                z = ps_z[:, j % GR % ZB, 0:HALF]
                nc.tensor.matmul(z[0:g.D, :], g.Wc1T[:, :], ea_T[:, 0, :], start=True, stop=True)
                nc.tensor.matmul(z[g.D:P, :], g.Wc1T[:, :], ea_T[:, 1, :], start=True, stop=True).then_inc(z_done, 1)

            def second(j, G):
                pe.wait_ge(sp_ready, G + (j + 1))
                out = ps_e[:, j % 2, 0:GT * g.D]
                nc.tensor.matmul(out, g.ones3[:, :], g.bc2p[:, :, :].rearrange("o t d -> o (t d)"),
                                 start=True, stop=False, skip_group_check=True)
                tiles = out.rearrange("p (t d) -> p t d", d=g.D)
                for i in range(MID):
                    nc.tensor.matmul(tiles[:, i:GT:MID + 1, :], sp_y[:, j, i * P:(i + 1) * P], g.Wc2d[:, :, :],
                                     start=False, stop=False, skip_group_check=True)
                for k in range(2):
                    last = nc.tensor.matmul(tiles[k * g.D:(k + 1) * g.D, MID, :], sp_y[:, j, MID * P:HALF],
                                            g.Wc2d[:, k, :], start=False, stop=True, skip_group_check=True)
                last.then_inc(h_done, 1)

            def sum_up(j, G, u):
                pe.wait_ge(msg_ready, G + (j + 1 + GR))
                if j == 0:
                    pe.wait_ge(seg_ready, u + 1)
                for i in range(GT):
                    s = j * GT + i
                    last = nc.tensor.matmul(ps_seg[:, 0:g.D], oh[:, s, :], msg[:, s, :],
                                            start=(s == 0), stop=(s == CT - 1))
                last.then_inc(seg_group, 1)

            pe.sem_inc(turned, GR)
            pe.sem_inc(seg_group, GR)
            turn(0, 0, 16)
            first(0, 0)
            turn(1, 0, 16)
            for c, w, u in each_unit(pe, g, "pe_unit1"):
                if c is None:
                    continue
                G = pe.snap(u * GR)
                for j in range(GR):
                    first(j + 1, G)
                    if j + 2 < GR:
                        turn(j + 2, G, u * 16 + 16)
                    else:
                        turn(j + 2, G, u * 16 + 32)
                    if j > 0:
                        sum_up(j - 1, G, u)
                    second(j, G)
                sum_up(GR - 1, G, u)


def node_phase1(nc, g):
    PAIRS = g.NB // 2
    L = range(2)
    T = LANE_TILES
    C = [t * g.D for t in T]
    AT = [t * g.D for t in LANE_AT]
    ALL = sum(C)
    assert 2 * g.D == P and max(C) <= BANK
    with ExitStack() as ctx:
        def sb(name, shape, dt=F32):
            return [ctx.enter_context(nc.sbuf_tensor(f"{name}{h}", shape(h), dt)) for h in L]

        def ps(name):
            return [ctx.enter_context(nc.psum_tensor(f"{name}{h}", [P, BANK], F32)) for h in L]

        def sem(name):
            return [ctx.enter_context(nc.semaphore(f"{name}{h}")) for h in L]

        def cols(h):
            return [P, C[h]]

        def tiles(h):
            return [P, T[h], g.D]

        cf = sb("cf_in_sb", cols)
        cT = sb("cT", cols)
        y_cap = sb("y_cap1", cols)
        e_y = sb("e_y1", cols)
        q = sb("q1", cols)
        sp_y = sb("sp_y1", cols)
        r = sb("r1", tiles)
        d = sb("d1", tiles)
        sq = sb("sq1", tiles)
        stat = sb("stat1", lambda h: [P, 6, T[h]])
        ps_c = ps("ps_c")
        ps_z = ps("ps_z1_")
        ps_y = ps("ps_y")

        cf_in = sem("cf_in")
        c_turned = sem("c_turned")
        c_copied = sem("c_copied")
        z_done = sem("z_done2")
        capped = sem("capped2")
        exp_done = sem("exp_done2")
        log_done = sem("log_done2")
        sp_ready = sem("sp_ready2")
        y_done = sem("y_done2")
        r_ready = sem("r_ready2")
        ln_step = sem("ln_step1")
        std_ready = sem("std_ready1")
        stored = ctx.enter_context(nc.semaphore("stored"))

        cf_v = g.cf[0:P * g.NT, :].rearrange("(p t) d -> p (t d)", t=g.NT)
        P16 = (P - 1) // 16 * 16
        out_v = g.out[0:(P - 1) * g.NT, :].rearrange("(p t) d -> p (t d)", t=g.NT)
        block = ctx.enter_context(nc.Block())

        @block.sync
        def _(sp):
            def load(v):
                for h in L:
                    sp.dma_start(cf[h][:, :], cf_v[:, bass.ds(v * ALL + AT[h], C[h])]).then_inc(cf_in[h], 16)

            def store(v):
                for h in L:
                    sp.wait_ge(ln_step[h], v * LN_STEPS + (LN_STEPS + 1))
                at = bass.ds(held(sp, v * ALL), ALL)
                sp.dma_start(out_v[0:P16, at], g.xres[0:P16, at]).then_inc(stored, 16)
                sp.dma_start(out_v[P16:P - 1, at], g.xres[P16:P - 1, at]).then_inc(stored, 16)

            load(0)
            for h in L:
                sp.wait_ge(c_turned[h], 1)
            load(1)
            with sp.Fori(0, PAIRS - 2) as v:
                for h in L:
                    sp.wait_ge(c_turned[h], v + 2)
                load(v + 2)
                store(v)
            store(PAIRS - 2)
            store(PAIRS - 1)
            left = g.N - (P - 1) * g.NT
            sp.dma_start(g.out[(P - 1) * g.NT:g.N, :].rearrange("t d -> (t d)").unsqueeze(0),
                         g.xres[P - 1:P, 0:left * g.D]).then_inc(stored, 16)
            sp.wait_ge(stored, 16 * (2 * PAIRS + 1))

        @block.tensor
        def _(pe):
            def turn(v):
                for h in L:
                    pe.wait_ge(cf_in[h], (v + 1) * 16)
                    pe.wait_ge(c_copied[h], v + 1)
                    for k in range(T[h] // 2):
                        last = nc.tensor.transpose(ps_c[h][:, k * P:(k + 1) * P], cf[h][:, k * P:(k + 1) * P],
                                                   g.identF[:, :])
                    last.then_inc(c_turned[h], 1)

            def first_product(v):
                for h in L:
                    pe.wait_ge(c_copied[h], v + 2)
                    nc.tensor.matmul(ps_z[h][:, 0:C[h]], g.V2d[:, :, :].rearrange("p a d -> p (a d)"), cT[h][:, :],
                                     start=True, stop=True).then_inc(z_done[h], 1)

            def second_product(v):
                for h in L:
                    pe.wait_ge(r_ready[h], v + 1)
                    pe.wait_ge(sp_ready[h], v + 1)
                    nc.tensor.matmul(ps_y[h][:, 0:C[h]], g.ones3[:, :], g.v3p[:, 0:T[h], :].rearrange("o t d -> o (t d)"),
                                     start=True, stop=False, skip_group_check=True)
                    for k in range(T[h] // 2):
                        two = slice(k * P, (k + 1) * P)
                        last = nc.tensor.matmul(ps_y[h][:, two], sp_y[h][:, two],
                                                g.V3d[:, :, :].rearrange("p a d -> p (a d)"),
                                                start=False, stop=(k == T[h] // 2 - 1), skip_group_check=True)
                    last.then_inc(y_done[h], 1)

            for h in L:
                pe.sem_inc(c_copied[h], 1)
            turn(0)
            with pe.Fori(0, PAIRS - 1) as v:
                first_product(v)
                turn(v + 1)
                second_product(v)
            first_product(PAIRS - 1)
            second_product(PAIRS - 1)

        @block.scalar
        def _(act):
            def copy_c(v):
                for h in L:
                    act.wait_ge(c_turned[h], v + 1)
                    nc.scalar.copy(cT[h][:, :], ps_c[h][:, 0:C[h]]).then_inc(c_copied[h], 1)

            def root(v):
                act.preload_act_table_set("sqrt_and_others")
                for h in L:
                    act.wait_ge(ln_step[h], v * LN_STEPS + (LN_SQRT + 1))
                    nc.scalar.sqrt(stat[h][:, 4, :], stat[h][:, 3, :]).then_inc(std_ready[h], 1)

            def exp_log(v):
                act.preload_act_table_set("natural_log_exp_and_others")
                for h in L:
                    act.wait_ge(capped[h], v + 1)
                    nc.scalar.activation(e_y[h][:, :], y_cap[h][:, :], ACT.Exp).then_inc(exp_done[h], 1)
                for h in L:
                    act.wait_ge(exp_done[h], v + 1)
                    nc.scalar.activation(q[h][:, :], e_y[h][:, :], ACT.Ln, bias=1.0).then_inc(log_done[h], 1)

            copy_c(0)
            exp_log(0)
            copy_c(1)
            with act.Fori(0, PAIRS - 2) as v:
                exp_log(v + 1)
                root(v)
                copy_c(v + 2)
            exp_log(PAIRS - 1)
            root(PAIRS - 2)
            root(PAIRS - 1)

        @block.vector
        def _(dve):
            def x_cols(v):
                return [g.xres[:, bass.ds(held(dve, v * ALL + AT[h]), C[h])] for h in L]

            def cap(v):
                for h in L:
                    dve.wait_ge(z_done[h], v + 1)
                    nc.vector.tensor_scalar(y_cap[h][:, :], ps_z[h][:, 0:C[h]], g.v2h[:, 0:1], CAP,
                                            ALU.add, ALU.min).then_inc(capped[h], 1)

            def softplus(v):
                for h in L:
                    dve.wait_ge(log_done[h], v + 1)
                    nc.vector.scalar_tensor_tensor(out=sp_y[h][:, :], in0=ps_z[h][:, 0:C[h]], scalar=g.v2h[:, 0:1],
                                                   in1=q[h][:, :], op0=ALU.add, op1=ALU.max).then_inc(sp_ready[h], 1)

            def residual(v):
                x = x_cols(v)
                for h in L:
                    dve.wait_ge(y_done[h], v + 1)
                    dve.wait_ge(ln_step[h], v * LN_STEPS + 1)
                    nc.vector.scalar_tensor_tensor(out=r[h][:, :, :].rearrange("p t d -> p (t d)"), in0=x[h], scalar=2.0,
                                                   in1=ps_y[h][:, 0:C[h]], op0=ALU.mult, op1=ALU.add).then_inc(r_ready[h], 1)

            def normalise(v, first, end):
                x = x_cols(v)
                steps = [layer_norm(nc, g, r[h][:, :, :], d[h][:, :, :], sq[h][:, :, :], stat[h],
                                    x[h].rearrange("p (t d) -> p t d", d=g.D)) for h in L]
                for k in range(first, end):
                    for h in L:
                        if k == 0:
                            dve.wait_ge(r_ready[h], v + 2)
                        elif k == LN_SQRT:
                            dve.wait_ge(std_ready[h], v + 1)
                        else:
                            dve.wait_ge(ln_step[h], v * LN_STEPS + (k + 1))
                        steps[h][k]().then_inc(ln_step[h], 1)

            for h in L:
                dve.sem_inc(ln_step[h], 1)
                dve.sem_inc(r_ready[h], 1)
            cap(0)
            softplus(0)
            residual(0)
            with dve.Fori(0, PAIRS - 1) as v:
                normalise(v, 0, 3)
                cap(v + 1)
                normalise(v, 3, LN_SQRT)
                softplus(v + 1)
                normalise(v, LN_SQRT, LN_STEPS)
                residual(v + 1)
            normalise(PAIRS - 1, 0, LN_STEPS)


def build(nc, ins, out):
    with ExitStack() as ctx:
        g = make_plan(nc, ctx, ins, out)
        prep_phase(nc, g)
        layer0_edges(nc, g)
        node_phase0(nc, g)
        layer1_edges(nc, g)
        node_phase1(nc, g)


_INS = ["x", "src", "dst", "edge_attr_128", "L0_gnn_W1", "L0_gnn_b1", "L0_gnn_W2", "L0_gnn_b2", "L1_gnn_W1",
        "L1_gnn_Wc1", "L1_gnn_bc1", "L1_gnn_Wc2", "L1_gnn_bc2", "L1_gnn_W2", "L1_gnn_b2", "L1_gnn_W3", "L1_gnn_b3"]


def kernel(**inputs):
    import numpy as _np
    import concourse.bacc as _bacc
    from concourse import mybir as _mybir
    from concourse.bass_utils import run_bass_kernel_spmd as _run

    nc = _bacc.Bacc("TRN2", target_bir_lowering=False, num_devices=1)
    arrays, aps = {}, {}
    for name in _INS:
        a = _np.ascontiguousarray(inputs[name])
        arrays[f"in_{name}_dram"] = a
        aps[name] = nc.dram_tensor(f"in_{name}_dram", a.shape, _mybir.dt.from_np(a.dtype), kind="ExternalInput").ap()
    out = nc.dram_tensor("out_0_dram", inputs["x"].shape, _mybir.dt.float32, kind="ExternalOutput").ap()
    build(nc, aps, out)
    r = _run(nc, [arrays], core_ids=[0])
    return r.results[0]["out_0_dram"]
```
